# Optimizing a Trainium2 kernel written in Bass

```python
import numpy as np
import jax
import jax.numpy as jnp

def _softmax(x, axis=-1):
    return jax.nn.softmax(x, axis=axis)

def _gelu(x):
    return jax.nn.gelu(x, approximate=True)

def _silu(x):
    return jax.nn.silu(x)

def _sigmoid(x):
    return jax.nn.sigmoid(x)

def _layernorm(x, axis=-1, eps=1e-05):
    m = jnp.mean(x, axis=axis, keepdims=True)
    v = jnp.var(x, axis=axis, keepdims=True)
    return (x - m) / jnp.sqrt(v + eps)

def _scatter_add(tgt, idx, src, axis=0):
    return tgt.at[idx].add(src)

def _segment_sum(src, seg, n):
    return jax.ops.segment_sum(src, seg, n)
kernel_name = 'mk_xattn_ffn_d1_seqx_r4_c8221f'

def setup_inputs(seed: int=0):
    np.random.seed(seed)
    _w = jnp.asarray

    def _rec_inputs():
        import jax
        import jax.numpy as jnp
        _rk = jax.random.key(seed)
        x = -0.000125 + 0.9999 * jax.random.normal(jax.random.fold_in(_rk, 1), (8, 256, 512), jnp.float32)
        _lenS = 256 - jax.random.randint(jax.random.fold_in(_rk, 7), (8,), 0, max(1, 256 // 4) + 1, jnp.int32)
        _lenS2 = 256 - jax.random.randint(jax.random.fold_in(_rk, 8), (8,), 0, max(1, 256 // 4) + 1, jnp.int32)
        _ctx_2048P = jax.random.normal(jax.random.fold_in(_rk, 11), (8, 16, 512), jnp.float32)
        _ctx_2048c = jax.random.dirichlet(jax.random.fold_in(_rk, 511), 0.3 * jnp.ones((16,), jnp.float32), (8, 256))
        _ctx_2048t = jnp.einsum('bsk,bkd->bsd', _ctx_2048c, _ctx_2048P)
        _ctx_2048t = _ctx_2048t * jax.lax.rsqrt(jnp.mean(jnp.square(_ctx_2048t)) + 1e-12) * 0.953939
        ctx_2048 = 0.00139358 + 0.999369 * (_ctx_2048t + 0.3 * jax.random.normal(jax.random.fold_in(_rk, 611), (8, 256, 512), jnp.float32))
        return (x, ctx_2048)
    x, ctx_2048 = _rec_inputs()

    def _L0_xattn_setup():
        import jax, jax.numpy as jnp
        import numpy as np
        key = jax.random.key(seed)
        k = jax.random.split(key, 6)
        B, S, D, NKV = (4, 1024, 512, 64)
        inv = D ** (-0.5)
        return {'x': jax.random.normal(k[0], (B, S, D), jnp.float32), 'W_qkv': jax.random.normal(k[1], (3 * D, D), jnp.float32) * inv, 'W_o': jax.random.normal(k[2], (D, D), jnp.float32) * inv, 'beta_q': jnp.array(1.0, jnp.float32), 'beta_k': jnp.array(1.0, jnp.float32), 'gate': jnp.array(0.0, jnp.float32), 'log_tau': jnp.array(0.0, jnp.float32), 'K_mem': jax.random.normal(k[3], (B, NKV, D), jnp.float32), 'V_mem': jax.random.normal(k[4], (B, NKV, D), jnp.float32), 'clip_k': 54}
    _L0_xattn_all = _L0_xattn_setup()
    _L0_xattn_in = {k: v for k, v in _L0_xattn_all.items() if k in ('W_qkv', 'W_o', 'beta_q', 'beta_k', 'gate', 'log_tau')}
    del _L0_xattn_all

    def _L0_ffn_setup():
        import jax, jax.numpy as jnp
        import numpy as np
        from jax import lax
        H = 512
        I = 352
        E = 16
        TOP_K = 6
        IS = 2 * I

        def _swiglu(x, w13_, w2_):
            gu = x @ w13_.T
            g, u = jnp.split(gu, 2, axis=-1)
            return jax.nn.silu(g) * u @ w2_.T
        key = jax.random.key(seed)
        ks = jax.random.split(key, 6)
        return {'hidden_states': jax.random.normal(ks[0], (1, 512, H), jnp.float32), 'gate_w': jax.random.normal(ks[1], (E, H), jnp.float32) * 0.02, 'w13': jax.random.normal(ks[2], (E, 2 * I, H), jnp.float32) * 0.02, 'w2': jax.random.normal(ks[3], (E, H, I), jnp.float32) * 0.02, 'sw13': jax.random.normal(ks[4], (2 * IS, H), jnp.float32) * 0.02, 'sw2': jax.random.normal(ks[5], (H, IS), jnp.float32) * 0.02}
    _L0_ffn_all = _L0_ffn_setup()
    _L0_ffn_in = {k: v for k, v in _L0_ffn_all.items() if k in ('gate_w', 'w13', 'w2', 'sw13', 'sw2')}
    del _L0_ffn_all
    return {'x': x, 'ctx_2048': ctx_2048, 'L0_xattn_W_qkv': _L0_xattn_in['W_qkv'], 'L0_xattn_W_o': _L0_xattn_in['W_o'], 'L0_xattn_beta_q': _L0_xattn_in['beta_q'], 'L0_xattn_beta_k': _L0_xattn_in['beta_k'], 'L0_xattn_gate': _L0_xattn_in['gate'], 'L0_xattn_log_tau': _L0_xattn_in['log_tau'], 'L0_ffn_gate_w': _L0_ffn_in['gate_w'], 'L0_ffn_w13': _L0_ffn_in['w13'], 'L0_ffn_w2': _L0_ffn_in['w2'], 'L0_ffn_sw13': _L0_ffn_in['sw13'], 'L0_ffn_sw2': _L0_ffn_in['sw2']}

def reference(x, ctx_2048, L0_xattn_W_qkv, L0_xattn_W_o, L0_xattn_beta_q, L0_xattn_beta_k, L0_xattn_gate, L0_xattn_log_tau, L0_ffn_gate_w, L0_ffn_w13, L0_ffn_w2, L0_ffn_sw13, L0_ffn_sw2):
    import jax
    import jax.numpy as jnp

    def _L0_xattn_ref(x, W_qkv, W_o, beta_q, beta_k, gate, log_tau, K_mem, V_mem, clip_k):
        import jax, jax.numpy as jnp
        import numpy as np
        D = x.shape[-1]
        scale = D ** (-0.5)
        qkv = x @ W_qkv.T
        Q = qkv[..., :D]
        alpha = jax.nn.sigmoid(gate)
        tau = jnp.exp(log_tau)
        coef = (alpha * beta_q + (1.0 - alpha) * beta_k) * scale * tau
        scores = coef * jnp.einsum('bsd,bnd->bsn', Q, K_mem)
        scores = scores - jnp.max(scores, axis=-1, keepdims=True)
        thr = jax.lax.top_k(scores, clip_k)[0][..., -1:]
        scores = jnp.where(scores < thr, -jnp.inf, scores)
        att = jax.nn.softmax(scores, axis=-1)
        out = jnp.einsum('bsn,bnd->bsd', att, V_mem)
        return out @ W_o.T

    def _L0_ffn_ref(hidden_states, gate_w, w13, w2, sw13, sw2):
        import jax, jax.numpy as jnp
        import numpy as np
        from jax import lax
        H = 512
        I = 352
        E = 16
        TOP_K = 6
        IS = 2 * I

        def _swiglu(x, w13_, w2_):
            gu = x @ w13_.T
            g, u = jnp.split(gu, 2, axis=-1)
            return jax.nn.silu(g) * u @ w2_.T
        B, S, Hd = hidden_states.shape
        x = hidden_states.reshape(-1, Hd)
        T = x.shape[0]
        scores = jax.nn.softmax(x @ gate_w.T, axis=-1)
        topk_w, topk_ids = lax.top_k(scores, TOP_K)
        topk_w = topk_w / (topk_w.sum(-1, keepdims=True) + 1e-20)
        combine = jnp.einsum('tk,tke->te', topk_w, jax.nn.one_hot(topk_ids, E, dtype=topk_w.dtype))

        def body(acc, ew):
            w13_e, w2_e, c_e = ew
            y = _swiglu(x, w13_e, w2_e)
            return (acc + c_e[:, None] * y, None)
        out, _ = lax.scan(body, jnp.zeros_like(x), (w13, w2, combine.T))
        out = out + _swiglu(x, sw13, sw2)
        return out.reshape(B, S, Hd)
    x = x + _L0_xattn_ref(_layernorm(x, axis=-1), L0_xattn_W_qkv, L0_xattn_W_o, L0_xattn_beta_q, L0_xattn_beta_k, L0_xattn_gate, L0_xattn_log_tau, ctx_2048, ctx_2048, 54)
    x = x + _L0_ffn_ref(_layernorm(x, axis=-1), L0_ffn_gate_w, L0_ffn_w13, L0_ffn_w2, L0_ffn_sw13, L0_ffn_sw2)
    return x

_drawn_inputs = setup_inputs


def setup_inputs(seed=0):
    import zlib

    import numpy as np

    out = dict(_drawn_inputs(seed))
    spreads = {}
    factors = {'L0_ffn_gate_w': 4.829, 'L0_ffn_w13': 3.842, 'L0_ffn_w2': 3.849}
    for name, (base, spread) in spreads.items():
        noise = np.random.default_rng([zlib.crc32(name.encode()), seed]).standard_normal(out[name].shape)
        drawn = base * np.exp(spread * noise) if base else spread * noise
        out[name] = jnp.asarray(drawn.astype(out[name].dtype))
    for name, factor in factors.items():
        out[name] = (out[name] * factor).astype(out[name].dtype)
    return out
```

```python
from contextlib import ExitStack

import concourse.bass as bass
from concourse import mybir

F32 = mybir.dt.float32
F32R = mybir.dt.float32r
BF16 = mybir.dt.bfloat16
I32 = mybir.dt.int32
ALU = mybir.AluOpType
ACT = mybir.ActivationFunctionType
AX = mybir.AxisListType

P = 128
BATCH, SEQ, D = 8, 256, 512
KEEP = 54
TOKENS = BATCH * SEQ
TILES = TOKENS // P
TPB = SEQ // P
KC = D // P
NC = SEQ // P
EXPERTS, TOPK = 16, 6
INNER = 352
HC = 3
HPAD = HC * P
ROUTED = TOKENS * TOPK // P + EXPERTS
BLOCKS = TILES + ROUTED + TILES
SETS = EXPERTS + 2
W13 = KC * 2 * INNER
WSET = W13 + HC * D
SLOT = 2 * WSET
SLOTS = 3
UNROLL = 4
RING = 8
EPS = 1e-5
SCALE = float(D) ** -0.5
ROUNDS = -(-KEEP // 8)
LOWEST = -3.0e38
SENTINEL, TAKEN = -1.0, -2.0


class Steps:

    def __init__(self, eng, sem):
        self.eng, self.sem, self.base, self.n = eng, sem, 0, 0
        
    def did(self, instruction):
        instruction.then_inc(self.sem, 1)
        self.n += 1

    def order(self):
        self.eng.wait_ge(self.sem, self.base + self.n)

    def alone(self):
        self.eng.nop(nofuse=True)

    def enter(self, i, first, per):
        self.before, self.per, self.base, self.n = self.n, per, i * per + (self.n - first * per), 0

    def leave(self, count):
        assert self.n == self.per, f"{self.sem}: {self.n} steps in an iteration, not {self.per}"
        self.base, self.n = 0, self.before + count * self.per


def xattn_moe(nc, x, ctx_n, ctx_t, wq_t, wo_t, beta_q, beta_k, gate, log_tau, gate_w_t,
              w13, w2, sw13, sw2, out):
    with ExitStack() as stack:
        def sb(name, shape, dt=F32):
            return stack.enter_context(nc.sbuf_tensor(name, shape, dt))

        def sem(name):
            return stack.enter_context(nc.semaphore(name))

        xn2_dram = nc.dram_tensor("xn2_dram", [TOKENS, D], F32, kind="Internal")
        sorted_dram = nc.dram_tensor("sorted_dram", [ROUTED * P, D], F32, kind="Internal")
        y_dram = nc.dram_tensor("y_dram", [ROUTED * P, D], F32, kind="Internal")

        acc = sb("acc", [P, TILES, D])
        raw = sb("raw", [P, WSET])
        slots = sb("slots", [P, SLOTS * SLOT], F32R)
        tail = sb("tail", [P, 5248], F32R)
        arena = sb("arena", [P, 4096])
        tab = sb("tab", [P, 1792])

        def carve(tensor, at, *dims):
            n = 1
            for d in dims:
                n *= d
            ap = tensor[:, at:at + n]
            names = "abc"[:len(dims)]
            if len(dims) > 1:
                ap = ap.rearrange(f"p ({' '.join(names)}) -> p {' '.join(names)}",
                                  **dict(zip(names[1:], dims[1:])))
            return ap, at + n

        at = SLOT
        pairs = {}
        for name, dims in (("wq", (KC, D)), ("wo", (KC, D)), ("xt", (KC, SEQ)), ("cn", (NC, D)),
                           ("ct", (KC, SEQ)), ("qt", (KC, SEQ))):
            hi, at = carve(slots, at, *dims)
            lo, at = carve(slots, at, *dims)
            pairs[name] = (hi, lo)
        assert at <= SLOTS * SLOT
        at = 0
        for name, dims in (("pt", (NC, SEQ)), ("ot", (KC, SEQ)), ("x2", (KC, SEQ)), ("gw", (KC, EXPERTS))):
            hi, at = carve(tail, at, *dims)
            lo, at = carve(tail, at, *dims)
            pairs[name] = (hi, lo)
        wq, wo, xt, cn, ct, qt = (pairs[k] for k in ("wq", "wo", "xt", "cn", "ct", "qt"))
        pt, ot, x2, gw = (pairs[k] for k in ("pt", "ot", "x2", "gw"))
        xn, at = carve(arena, 0, TPB, D)
        xn2, at = carve(arena, at, TPB, D)
        sc, at = carve(arena, at, TPB, SEQ)
        left, at = carve(arena, at, TPB, SEQ)
        shifted, at = carve(arena, at, TPB, SEQ)
        probs, at = carve(arena, at, TPB, SEQ)
        raw_q, at = carve(raw, 0, KC, D)
        raw_o, at = carve(raw, at, KC, D)
        raw_cn, at = carve(raw, 0, NC, D)
        raw_ct, at = carve(raw, at, KC, SEQ)
        bx = [None, None]
        at = 0
        for j in range(2):
            hi, at = carve(tail, at, KC, P)
            lo, at = carve(tail, at, KC, P)
            bx[j] = (hi, lo)
        hth, at = carve(tail, at, HC, P)
        htl, at = carve(tail, at, HC, P)
        xb = [None] * UNROLL
        at = 0
        for j in range(UNROLL):
            xb[j], at = carve(arena, at, D)
        ys = [None] * 2
        for j in range(2):
            ys[j], at = carve(arena, at, D)
        hid, at = carve(arena, at, HPAD)
        silu, at = carve(arena, at, INNER)
        assert at <= 4096
        ring = [raw[:, r * D:(r + 1) * D] for r in range(RING)]

        zeros = tab[:, 0:D]
        cmp_block = tab[:, 0:ROUTED * EXPERTS].rearrange("p (i e) -> p i e", e=EXPERTS)
        ident = sb("ident", [P, P])
        upper = sb("upper", [P, P], BF16)
        ones = sb("ones", [P, P], BF16)
        raw_gw = sb("raw_gw", [P, KC, EXPERTS])
        scal = sb("scal", [P, 4])
        cf = sb("cf", [P, 8])
        coef = cf[:, 7:8]
        neghalf = sb("neghalf", [P, TPB])
        stats1 = sb("stats1", [P, TPB, 6])
        stats2 = sb("stats2", [P, TPB, 6])
        mv1 = sb("mv1", [P, TPB, 2])
        mv2 = sb("mv2", [P, TPB, 2])
        ve1 = sb("ve1", [P, TPB])
        ve2 = sb("ve2", [P, TPB])
        rstd1 = sb("rstd1", [P, TPB])
        rstd2 = sb("rstd2", [P, TPB])
        top8 = sb("top8", [P, TPB, 8])
        negmax = sb("negmax", [P, TPB])
        thr = sb("thr", [P, TPB])
        psums = sb("psums", [P, TPB])
        rinv = sb("rinv", [P, TILES])
        rneg = sb("rneg", [P, TPB])
        rexp = sb("rexp", [P, TPB, EXPERTS])
        rsum = sb("rsum", [P, TPB])
        rrec = sb("rrec", [P, TPB])
        rp = sb("rp", [P, TPB, EXPERTS + 2])
        rq = sb("rq", [P, TPB, EXPERTS + 2])
        rtop = sb("rtop", [P, TPB, 8])
        rwsum = sb("rwsum", [P, TPB])
        rwrec = sb("rwrec", [P, TPB])
        sel = sb("sel", [P, TILES, EXPERTS], BF16)
        comb = sb("comb", [P, TILES, EXPERTS])
        run = sb("run", [P, TILES, EXPERTS])
        six_t = sb("six_t", [P, TILES, EXPERTS])
        pick = sb("pick", [P, TILES, EXPERTS])
        blocks_m = sb("blocks_m", [P, EXPERTS])
        nblk = sb("nblk", [P, EXPERTS])
        nblk1 = sb("nblk1", [P, EXPERTS])
        ends = sb("ends", [P, EXPERTS])
        starts = sb("starts", [P, EXPERTS])
        posn = sb("posn", [P, TILES, EXPERTS])
        cmp_e = posn
        delta = sb("delta", [P, EXPERTS])
        blk_i = sb("blk_i", [P, ROUTED])
        seq_f = sb("seq_f", [P, ROUTED])
        slot_f = sb("slot_f", [P, ROUTED])
        idx = sb("idx", [P, TILES, TOPK], I32)
        wgt = sb("wgt", [P, TILES, TOPK])
        idx_now = [sb(f"idx_now{j}", [P, TOPK], I32) for j in range(UNROLL)]
        slot_tab = sb("slot_tab", [1, BLOCKS], I32)
        ready_tab = sb("ready_tab", [1, BLOCKS], I32)
        end_tab = sb("end_tab", [1, EXPERTS], I32)

        ps = stack.enter_context(nc.psum_tensor("ps", [P, 8, 512], F32))
        ps_xt = ps[:, 0:2, :].rearrange("p a (b n) -> p (a b) n", n=SEQ)
        ps_qo = ps[:, 2:4, :].rearrange("p a (b n) -> p (a b) n", n=SEQ)
        ps_sc = ps[:, 4, :].rearrange("p (t n) -> p t n", n=SEQ)
        ps_pt = ps[:, 5, :].rearrange("p (c n) -> p c n", n=SEQ)
        ps_lg = ps[:, 5, 0:TPB * EXPERTS].rearrange("p (t e) -> p t e", e=EXPERTS)
        ps_y = [ps[:, 6, :], ps[:, 7, :]]
        ps_rank = ps[:, 4, 0:TILES * EXPERTS].rearrange("p (t e) -> p t e", e=EXPERTS)
        ps_tot = ps[:, 5, 0:EXPERTS]
        ps_bx = ps[:, 0, :].rearrange("p (c n) -> p c n", n=P)
        ps_ht = ps[:, 1, 0:HPAD].rearrange("p (c n) -> p c n", n=P)
        ps_g = ps[:, 2, 0:INNER]
        ps_u = ps[:, 3, 0:INNER]

        x_in = [sem("x_in0"), sem("x_in1"), sem("x_in_rest")]
        wqo_in = sem("wqo_in")
        small_in = sem("small_in")
        ctx_t_in = sem("ctx_t_in")
        ctx_n_in = sem("ctx_n_in")
        zeros_made = sem("zeros_made")
        zero_filled = sem("zero_filled")
        consts_made = sem("consts_made")
        pool_step = sem("pool_step")
        dve_step = sem("dve_step")
        act_step = sem("act_step")
        wqo_hi = sem("wqo_hi")
        wqo_split = sem("wqo_split")
        coef_exp = sem("coef_exp")
        coef_ready = sem("coef_ready")
        ln1_var = sem("ln1_var")
        ln2_var = sem("ln2_var")
        ln1_rstd = sem("ln1_rstd")
        ln2_rstd = sem("ln2_rstd")
        xn_ready = sem("xn_ready")
        xt_mm = sem("xt_mm")
        xt_hi = sem("xt_hi")
        xt_lo = sem("xt_lo")
        q_mm = sem("q_mm")
        q_hi = sem("q_hi")
        q_lo = sem("q_lo")
        ct_split = sem("ct_split")
        cn_split = sem("cn_split")
        sc_mm = sem("sc_mm")
        sc_taken = sem("sc_taken")
        max_ready = sem("max_ready")
        exp_ready = sem("exp_ready")
        probs_ready = sem("probs_ready")
        pt_mm = sem("pt_mm")
        pt_hi = sem("pt_hi")
        pt_lo = sem("pt_lo")
        o_mm = sem("o_mm")
        o_hi = sem("o_hi")
        o_lo = sem("o_lo")
        y_mm = sem("y_mm")
        x1_ready = sem("x1_ready")
        xn2_ready = sem("xn2_ready")
        xn2_stored = sem("xn2_stored")
        x2_mm = sem("x2_mm")
        x2_hi = sem("x2_hi")
        x2_lo = sem("x2_lo")
        lg_mm = sem("lg_mm")
        rmax_ready = sem("rmax_ready")
        rexp_ready = sem("rexp_ready")
        sel_ready = sem("sel_ready")
        rank_mm = sem("rank_mm")
        idx_ready = sem("idx_ready")
        tables_ready = sem("tables_ready")
        w_in = sem("w_in")
        w_ready = sem("w_ready")
        xb_in = [sem(f"xb_in{j}") for j in range(UNROLL)]
        scattered = [sem(f"scattered{j}") for j in range(UNROLL)]
        bx_mm = sem("bx_mm")
        bx_hi = sem("bx_hi")
        bx_lo = sem("bx_lo")
        gu_mm = sem("gu_mm")
        silu_ready = sem("silu_ready")
        hid_ready = sem("hid_ready")
        ht_mm = sem("ht_mm")
        ht_hi = sem("ht_hi")
        ht_lo = sem("ht_lo")
        down_mm = sem("down_mm")
        y_taken = sem("y_taken")
        y_stored = [sem(f"y_stored{j}") for j in range(2)]
        gathered = [sem(f"gathered{r}") for r in range(RING)]
        row_added = sem("row_added")
        out_stored = sem("out_stored")

        block = stack.enter_context(nc.Block())

        def parts3(a, b):
            return ((a[0], b[0]), (a[0], b[1]), (a[1], b[0]))

        def f32(ap):
            return ap.bitcast(F32)

        ctx_t_v = ctx_t.rearrange("(b p) n -> b p n", p=P)
        ctx_n_v = ctx_n.rearrange("(b c p) n -> p b c n", c=NC, p=P)
        xn2_v = xn2_dram[:, :].rearrange("(t p) n -> p t n", p=P)
        sorted_v = sorted_dram[:, :].rearrange("(i p) n -> p i n", p=P)
        y_v = y_dram[:, :].rearrange("(i p) n -> p i n", p=P)
        out_v = out.rearrange("(t p) n -> p t n", p=P)
        x_v = x.rearrange("(t p) n -> p t n", p=P)

        @block.sync
        def _(sp):
            def load_ctx_t(b):
                sp.dma_start(raw_ct.rearrange("p c n -> p (c n)"), ctx_t_v[b, :, :] if isinstance(b, int)
                             else ctx_t_v[bass.ds(b, 1), :, :].rearrange("o p n -> p (o n)")).then_inc(ctx_t_in, 16)

            def load_ctx_n(b):
                sp.dma_start(raw_cn, ctx_n_v[:, b, :, :]).then_inc(ctx_n_in, 16)

            def store_xn2(b):
                sp.wait_ge(xn2_ready, 2 * b + 2)
                sp.dma_start(xn2_v[:, bass.ds(b * 2, 2), :], xn2).then_inc(xn2_stored, 16)

            sp.dma_start(acc[:, 0:2, :], x_v[:, 0:2, :]).then_inc(x_in[0], 16)
            sp.dma_start(raw_q.rearrange("p c n -> p (c n)"), wq_t).then_inc(wqo_in, 16)
            sp.dma_start(raw_o.rearrange("p c n -> p (c n)"), wo_t).then_inc(wqo_in, 16)
            for s, src in enumerate((beta_q, beta_k, gate, log_tau)):
                sp.dma_start(scal[:, s:s + 1], src[0, :].partition_broadcast(P)).then_inc(small_in, 16)
            sp.dma_start(raw_gw[:, :, :], gate_w_t.rearrange("(c p) e -> p c e", p=P)).then_inc(small_in, 16)
            for b in range(1, BATCH):
                sp.dma_start(acc[:, 2 * b:2 * b + 2, :], x_v[:, 2 * b:2 * b + 2, :]).then_inc(x_in[min(b, 2)], 16)
            sp.wait_ge(wqo_split, 2)
            load_ctx_t(0)
            load_ctx_n(0)
            sp.wait_ge(zeros_made, 1)
            for g in range(0, ROUTED, 8):
                sp.dma_start(sorted_v[:, g:g + 8, :],
                             zeros.unsqueeze(1).broadcast_to([P, 8, D])).then_inc(zero_filled, 16)
            sp.wait_ge(ct_split, 2)
            load_ctx_t(1)
            sp.wait_ge(cn_split, 2)
            load_ctx_n(1)
            with sp.Fori(0, BATCH - 2) as b:
                sp.wait_ge(ct_split, b * 2 + 4)
                load_ctx_t(b + 2)
                sp.wait_ge(cn_split, b * 2 + 4)
                load_ctx_n(b + 2)
                store_xn2(b)
            for b in range(BATCH - 2, BATCH):
                store_xn2(b)
            sp.wait_ge(xn2_stored, 16 * BATCH)

            def load_block(n, src, tile, j, free=True):
                if free:
                    sp.wait_ge(bx_mm, n - UNROLL + 1)
                sp.dma_start(xb[j], src[:, tile, :]).then_inc(xb_in[j], 16)

            sp.wait_ge(lg_mm, BATCH)
            sp.wait_ge(sel_ready, BATCH)
            for j in range(UNROLL):
                load_block(j, xn2_v, j, j, free=False)
            with sp.Fori(1, TILES // UNROLL) as g:
                for j in range(UNROLL):
                    n = g * UNROLL + j
                    sp.wait_ge(scattered[j], g * (16 * TOPK))
                    sp.nop(nofuse=True)
                    load_block(n, xn2_v, n, j)
            for j in range(UNROLL):
                sp.wait_ge(scattered[j], 16 * TOPK * TILES // UNROLL)
            with sp.Fori(4, 4 + 1) as g:
                for j in range(UNROLL):
                    load_block(g * UNROLL + j, sorted_v, g * UNROLL + (j - TILES), j)
            with sp.Fori(5, 4 + ROUTED // UNROLL) as g:
                for j in range(UNROLL):
                    n = g * UNROLL + j
                    load_block(n, sorted_v, n - TILES, j)
                    m = n - UNROLL
                    sp.wait_ge(y_taken, m + 1)
                    sp.dma_start(y_v[:, m - TILES, :], ys[j % 2]).then_inc(y_stored[j % 2], 16)
            for j in range(UNROLL):
                n, m = TILES + ROUTED + j, TILES + ROUTED - UNROLL + j
                load_block(n, xn2_v, j, j)
                sp.wait_ge(y_taken, m + 1)
                sp.dma_start(y_v[:, m - TILES, :], ys[j % 2]).then_inc(y_stored[j % 2], 16)
            with sp.Fori(1, TILES // UNROLL) as g:
                for j in range(UNROLL):
                    t = g * UNROLL + j
                    load_block(t + (TILES + ROUTED), xn2_v, t, j)
                    sp.wait_ge(row_added, (t + (1 - UNROLL)) * TOPK)
                    sp.dma_start(out_v[:, t - UNROLL, :], acc[:, t - UNROLL, :]).then_inc(out_stored, 16)
            for t in range(TILES - UNROLL, TILES):
                sp.wait_ge(row_added, (t + 1) * TOPK)
                sp.dma_start(out_v[:, t, :], acc[:, t, :]).then_inc(out_stored, 16)
            sp.wait_ge(out_stored, 16 * TILES)

        @block.tensor
        def _(pe):
            def scores(b):
                pe.wait_ge(q_lo, b + 1)
                pe.wait_ge(ct_split, b * 2 + 2)
                if not (isinstance(b, int) and b == 0):
                    pe.wait_ge(sc_taken, b)
                for t in range(TPB):
                    prods = [(q[:, c, t * P:(t + 1) * P], k[:, c, :])
                             for c in range(KC) for q, k in parts3(qt, ct)]
                    for n, (q, k) in enumerate(prods):
                        mm = pe.matmul(ps_sc[:, t, :], q, k, start=n == 0, stop=n == len(prods) - 1)
                mm.then_inc(sc_mm, 1)

            def transpose_x(b):
                pe.wait_ge(xn_ready, b * 2 + 2)
                for t in range(TPB):
                    for c in range(KC):
                        mm = pe.transpose(ps_xt[:, c, t * P:(t + 1) * P], xn[:, t, c * P:(c + 1) * P], ident[:, :])
                mm.then_inc(xt_mm, 1)

            def queries(b):
                pe.wait_ge(xt_lo, b + 1)
                for j in range(KC):
                    prods = [(w[:, c, j * P:(j + 1) * P], a[:, c, :])
                             for c in range(KC) for w, a in parts3(wq, xt)]
                    for n, (w, a) in enumerate(prods):
                        mm = pe.matmul(ps_qo[:, j, :], w, a, start=n == 0, stop=n == len(prods) - 1)
                mm.then_inc(q_mm, 1)

            def transpose_probs(b):
                pe.wait_ge(probs_ready, b * 2 + 2)
                for t in range(TPB):
                    for c in range(NC):
                        mm = pe.transpose(ps_pt[:, c, t * P:(t + 1) * P], probs[:, t, c * P:(c + 1) * P], ident[:, :])
                mm.then_inc(pt_mm, 1)

            def attend(b):
                pe.wait_ge(pt_lo, b + 1)
                pe.wait_ge(cn_split, b * 2 + 2)
                for j in range(KC):
                    prods = [(v[:, c, j * P:(j + 1) * P], a[:, c, :])
                             for c in range(NC) for v, a in parts3(cn, pt)]
                    for n, (v, a) in enumerate(prods):
                        mm = pe.matmul(ps_qo[:, j, :], v, a, start=n == 0, stop=n == len(prods) - 1)
                mm.then_inc(o_mm, 1)

            def project(b):
                pe.wait_ge(o_lo, b + 1)
                for t in range(TPB):
                    if not (isinstance(b, int) and b == 0):
                        pe.wait_ge(x1_ready, b * 2 + (t - 1))
                    prods = [(o[:, c, t * P:(t + 1) * P], w[:, c, :])
                             for c in range(KC) for o, w in parts3(ot, wo)]
                    for n, (o, w) in enumerate(prods):
                        mm = pe.matmul(ps_y[t], o, w, start=n == 0, stop=n == len(prods) - 1)
                    mm.then_inc(y_mm, 1)

            def transpose_x2(b):
                pe.wait_ge(xn2_ready, b * 2 + 2)
                for t in range(TPB):
                    for c in range(KC):
                        mm = pe.transpose(ps_xt[:, c, t * P:(t + 1) * P], xn2[:, t, c * P:(c + 1) * P], ident[:, :])
                mm.then_inc(x2_mm, 1)

            def logits(b):
                pe.wait_ge(x2_lo, b + 1)
                for t in range(TPB):
                    prods = [(a[:, c, t * P:(t + 1) * P], w[:, c, :])
                             for c in range(KC) for a, w in parts3(x2, gw)]
                    for n, (a, w) in enumerate(prods):
                        mm = pe.matmul(ps_lg[:, t, :], a, w, start=n == 0, stop=n == len(prods) - 1)
                mm.then_inc(lg_mm, 1)

            def iteration(b, first=False, last=False):
                scores(b)
                if not last:
                    if not first:
                        pe.wait_ge(x2_lo, b - 1) if not (isinstance(b, int) and b < 2) else None
                    transpose_x(b + 1)
                if not first:
                    project(b - 1)
                if not last:
                    if not first:
                        pe.wait_ge(o_lo, b)
                    queries(b + 1)
                if not first:
                    if last:
                        pe.wait_ge(x2_lo, b - 1)
                    transpose_x2(b - 1)
                    if not (isinstance(b, int) and b < 2):
                        pe.wait_ge(rexp_ready, b - 1)
                transpose_probs(b)
                if not last:
                    pe.wait_ge(q_lo, b + 2)
                attend(b)
                if not first:
                    logits(b - 1)

            pe.wait_ge(consts_made, 5)
            pe.wait_ge(wqo_split, 3)
            transpose_x(0)
            queries(0)
            iteration(0, first=True)
            iteration(1)
            with pe.Fori(2, BATCH - 2) as b:
                iteration(b)
            iteration(BATCH - 2)
            iteration(BATCH - 1, last=True)
            project(BATCH - 1)
            pe.wait_ge(x2_lo, BATCH - 1)
            transpose_x2(BATCH - 1)
            pe.wait_ge(rexp_ready, BATCH - 1)
            logits(BATCH - 1)

            pe.wait_ge(sel_ready, BATCH)
            flat = sel[:, :, :].rearrange("p t e -> p (t e)")
            flat_rank = ps_rank.rearrange("p t e -> p (t e)")
            pe.matmul(flat_rank, upper[:, :], flat, start=True, stop=False)
            for t in range(TILES - 1):
                rest = TILES - 1 - t
                pe.matmul(ps_rank[:, t + 1:TILES, :], ones[:, :], sel[:, t:t + 1, :].broadcast_to([P, rest, EXPERTS]),
                          start=False, stop=False)
            mm = pe.matmul(flat_rank, upper[:, 0:1].broadcast_to([P, P]), flat, start=False, stop=True)
            mm.then_inc(rank_mm, 1)
            for t in range(TILES):
                mm = pe.matmul(ps_tot, ones[:, :], sel[:, t, :], start=t == 0, stop=t == TILES - 1)
            mm.then_inc(rank_mm, 1)

            def block_transpose(n, j):
                pe.wait_ge(xb_in[j], ((n - j) // UNROLL + 1) * 16 if isinstance(n, int)
                           else n * (16 // UNROLL) + (16 - j * (16 // UNROLL)))
                if not (isinstance(n, int) and n == 0):
                    pe.wait_ge(bx_lo, n)
                for c in range(KC):
                    mm = pe.transpose(ps_bx[:, c, :], xb[j][:, c * P:(c + 1) * P], ident[:, :])
                mm.then_inc(bx_mm, 1)

            def gate_up(n, j, off):
                pe.wait_ge(bx_lo, n + 1)
                for c in range(KC):
                    for part, (a, weights) in enumerate(((bx[j % 2][0], (0, WSET)), (bx[j % 2][1], (0,)))):
                        for half, bank in ((0, ps_g), (1, ps_u)):
                            for w in weights:
                                at = w + c * 2 * INNER + half * INNER
                                mm = pe.matmul(bank, a[:, c, :], slots[:, bass.ds(off + at, INNER)],
                                               start=c == 0 and part == 0 and w == 0,
                                               stop=c == KC - 1 and part == 1)
                mm.then_inc(gu_mm, 1)

            def hidden_transpose(n):
                pe.wait_ge(hid_ready, n + 1)
                if not (isinstance(n, int) and n == 0):
                    pe.wait_ge(ht_lo, n)
                for c in range(HC):
                    mm = pe.transpose(ps_ht[:, c, :], hid[:, c * P:(c + 1) * P], ident[:, :])
                mm.then_inc(ht_mm, 1)

            def down(n, j, off):
                pe.wait_ge(ht_lo, n + 1)
                if not (isinstance(n, int) and n < 2):
                    pe.wait_ge(y_taken, n - 1)
                for c in range(HC):
                    for part, (a, weights) in enumerate(((hth, (0, WSET)), (htl, (0,)))):
                        for w in weights:
                            at = w + W13 + c * D
                            mm = pe.matmul(ps_y[j % 2], a[:, c, :], slots[:, bass.ds(off + at, D)],
                                           start=c == 0 and part == 0 and w == 0,
                                           stop=c == HC - 1 and part == 1)
                mm.then_inc(down_mm, 1)

            def slot_of(n):
                return pe.value_load(slot_tab[0:1, bass.ds(n, 1)], min_val=0, max_val=(SLOTS - 1) * SLOT)

            def group(g, first=False, static=None):
                before = static if static is not None else slot_of(g * UNROLL - 1)
                for j in range(UNROLL):
                    n = g * UNROLL + j
                    here = static
                    if static is None:
                        here = slot_of(n)
                        sets = pe.value_load(ready_tab[0:1, bass.ds(n, 1)], min_val=1, max_val=SETS)
                    block_transpose(n + 1, (j + 1) % UNROLL)
                    if not (first and j == 0):
                        hidden_transpose(n - 1)
                    if static is None:
                        pe.wait_ge(w_ready, sets)
                    gate_up(n, j, here)
                    if not (first and j == 0):
                        down(n - 1, j - 1, before)
                    before = here

            pe.wait_ge(w_ready, 1)
            block_transpose(0, 0)
            group(0, first=True, static=0)
            with pe.Fori(1, TILES // UNROLL) as g:
                group(g, static=0)
            pe.wait_ge(tables_ready, 1)
            with pe.Fori(TILES // UNROLL, BLOCKS // UNROLL - 1) as g:
                group(g)
            g = BLOCKS // UNROLL - 1
            last_slot = (SETS - 1) % SLOTS * SLOT
            for j in range(UNROLL):
                n = g * UNROLL + j
                if j + 1 < UNROLL:
                    block_transpose(n + 1, j + 1)
                hidden_transpose(n - 1)
                gate_up(n, j, last_slot)
                down(n - 1, j - 1, last_slot)
            hidden_transpose(BLOCKS - 1)
            down(BLOCKS - 1, UNROLL - 1, last_slot)

        @block.scalar
        def _(act):
            step = Steps(act, act_step)

            def hi(dst, src, done):
                act.activation(dst, src, ACT.Copy).then_inc(done, 1)

            def take_scores(b):
                act.wait_ge(sc_mm, b + 1)
                if not (isinstance(b, int) and b == 0):
                    act.wait_ge(probs_ready, b * 2)
                act.activation(sc, ps_sc, ACT.Copy, scale=coef).then_inc(sc_taken, 1)

            def exponent(b, t):
                act.wait_ge(max_ready, b * 2 + (t + 1))
                if t == 0 and not (isinstance(b, int) and b == 0):
                    act.wait_ge(pt_mm, b)
                step.did(act.activation(shifted[:, t, :], sc[:, t, :], ACT.Identity, bias=negmax[:, t:t + 1]))
                step.order()
                act.activation(probs[:, t, :], shifted[:, t, :], ACT.Exp).then_inc(exp_ready, 1)

            def iteration(b, first=False, last=False):
                take_scores(b)
                if not last:
                    act.wait_ge(xt_mm, b + 2)
                    act.wait_ge(q_mm, b + 1)
                    hi(xt[0], ps_xt, xt_hi)
                exponent(b, 0)
                exponent(b, 1)
                if not last:
                    act.wait_ge(q_mm, b + 2)
                    hi(qt[0], ps_qo, q_hi)
                if not first:
                    x2_part(b - 1)
                act.wait_ge(pt_mm, b + 1)
                if not first:
                    act.wait_ge(o_mm, b)
                hi(pt[0], ps_pt, pt_hi)
                act.wait_ge(o_mm, b + 1)
                if not first:
                    act.wait_ge(y_mm, b * 2)
                hi(ot[0], ps_qo, o_hi)
                if not first:
                    router_exp(b - 1)

            def x2_part(b):
                act.wait_ge(x2_mm, b + 1)
                if not (isinstance(b, int) and b == 0):
                    act.wait_ge(lg_mm, b)
                hi(x2[0], ps_xt, x2_hi)

            def router_exp(b):
                act.wait_ge(rmax_ready, b + 1)
                for t in range(TPB):
                    last = act.activation(rexp[:, t, :], ps_lg[:, t, :], ACT.Exp, bias=rneg[:, t:t + 1])
                last.then_inc(rexp_ready, 1)

            act.wait_ge(wqo_in, 32)
            hi(wq[0], raw_q, wqo_hi)
            hi(wo[0], raw_o, wqo_hi)
            act.wait_ge(small_in, 16 * 5)
            hi(gw[0], raw_gw[:, :, :], wqo_hi)
            act.activation(cf[:, 0:1], scal[:, 2:3], ACT.Exp, scale=-1.0)
            act.activation(cf[:, 1:2], scal[:, 3:4], ACT.Exp).then_inc(coef_exp, 1)
            act.wait_ge(xt_mm, 1)
            hi(xt[0], ps_xt, xt_hi)
            act.wait_ge(q_mm, 1)
            hi(qt[0], ps_qo, q_hi)
            act.wait_ge(coef_ready, 1)
            iteration(0, first=True)
            step_count = 2
            iteration(1)
            with act.Fori(2, BATCH - 2) as b:
                step.enter(b, 2, step_count)
                iteration(b)
                step.leave(BATCH - 4)
            iteration(BATCH - 2)
            iteration(BATCH - 1, last=True)
            x2_part(BATCH - 1)
            router_exp(BATCH - 1)

            def tokens_hi(n, j):
                act.wait_ge(bx_mm, n + 1)
                if not (isinstance(n, int) and n < 2):
                    act.wait_ge(gu_mm, n - 1)
                hi(bx[j % 2][0], ps_bx, bx_hi)

            def hidden_hi(n):
                act.wait_ge(ht_mm, n + 1)
                if not (isinstance(n, int) and n == 0):
                    act.wait_ge(down_mm, n)
                hi(hth, ps_ht, ht_hi)

            def gate_silu(n):
                act.wait_ge(gu_mm, n + 1)
                if not (isinstance(n, int) and n == 0):
                    act.wait_ge(hid_ready, n)
                act.activation(silu, ps_g, ACT.Silu).then_inc(silu_ready, 1)

            def group(g, first=False, last=False):
                for j in range(UNROLL):
                    n = g * UNROLL + j
                    if not (last and j == UNROLL - 1):
                        tokens_hi(n + 1, j + 1)
                    if not (first and j == 0):
                        hidden_hi(n - 1)
                    gate_silu(n)

            tokens_hi(0, 0)
            group(0, first=True)
            with act.Fori(1, BLOCKS // UNROLL - 1) as g:
                group(g)
            group(BLOCKS // UNROLL - 1, last=True)
            hidden_hi(BLOCKS - 1)

        @block.vector
        def _(dve):
            step = Steps(dve, dve_step)

            def lo(dst, src, high, ready, count, done):
                dve.wait_ge(ready, count)
                dve.tensor_tensor(dst, src, f32(high), ALU.subtract).then_inc(done, 1)

            def norm_stats(b, stats, mv, ve, out_sem):
                step.alone()
                for t in range(TPB):
                    step.did(dve.bn_stats(stats[:, t, :], acc[:, b * 2 + t, :]))
                step.order()
                step.alone()
                for t in range(TPB):
                    step.did(dve.bn_aggr(mv[:, t, :], stats[:, t, :]))
                step.order()
                dve.tensor_scalar(ve[:, :], mv[:, :, 1], EPS, None, ALU.add).then_inc(out_sem, 1)

            def norm_apply(b, dst, mv, rstd, ready, done):
                dve.wait_ge(ready, b + 1)
                for t in range(TPB):
                    dve.tensor_scalar(dst[:, t, :], acc[:, b * 2 + t, :], mv[:, t, 0:1], rstd[:, t:t + 1],
                                      ALU.subtract, ALU.mult).then_inc(done, 1)

            def ln1_stats(b):
                if isinstance(b, int) and b <= 2:
                    dve.wait_ge(x_in[b], 16 if b < 2 else 16 * (BATCH - 2))
                norm_stats(b, stats1, mv1, ve1, ln1_var)

            def ln1_apply(b):
                if not (isinstance(b, int) and b == 0):
                    dve.wait_ge(xt_mm, b)
                norm_apply(b, xn, mv1, rstd1, ln1_rstd, xn_ready)

            def ln2_apply(b):
                if not (isinstance(b, int) and b == 0):
                    dve.wait_ge(x2_mm, b)
                    dve.wait_ge(xn2_stored, b * 16)
                norm_apply(b, xn2, mv2, rstd2, ln2_rstd, xn2_ready)

            def top_round(r):
                src = sc if r == 0 else left
                step.order()
                step.alone()
                for t in range(TPB):
                    step.did(dve.max(top8[:, t, :], src[:, t, :]))
                step.order()
                step.alone()
                if r == 0:
                    for t in range(TPB):
                        dve.tensor_scalar(negmax[:, t:t + 1], top8[:, t, 0:1], -1.0, None, ALU.mult)\
                           .then_inc(max_ready, 1)
                if r < ROUNDS - 1:
                    for t in range(TPB):
                        step.did(dve.match_replace(left[:, t, :], top8[:, t, :], src[:, t, :], LOWEST))

            def masked_probs(b):
                at = (KEEP - 1) % 8
                dve.wait_ge(max_ready, b * 2 + 2)
                step.did(dve.tensor_tensor(thr[:, :], top8[:, :, at], negmax[:, :], ALU.add))
                step.order()
                for t in range(TPB):
                    dve.wait_ge(exp_ready, b * 2 + (t + 1))
                    dve.scalar_tensor_tensor(out=probs[:, t, :], in0=shifted[:, t, :], scalar=thr[:, t:t + 1],
                                             in1=probs[:, t, :], op0=ALU.is_ge, op1=ALU.mult,
                                             accum_out=psums[:, t:t + 1]).then_inc(probs_ready, 1)
                dve.wait_ge(probs_ready, b * 2 + 2)
                step.did(dve.reciprocal(rinv[:, bass.ds(b * 2, 2)], psums[:, :]))

            def residual(b):
                step.order()
                for t in range(TPB):
                    dve.wait_ge(y_mm, b * 2 + (t + 1))
                    dve.scalar_tensor_tensor(out=acc[:, b * 2 + t, :], in0=ps_y[t], scalar=rinv[:, bass.ds(b * 2 + t, 1)],
                                             in1=acc[:, b * 2 + t, :], op0=ALU.mult, op1=ALU.add)\
                       .then_inc(x1_ready, 1)
                dve.wait_ge(x1_ready, b * 2 + 2)

            def router(b):
                dve.wait_ge(lg_mm, b + 1)
                step.order()
                dve.tensor_reduce(rneg[:, :], ps_lg, AX.X, ALU.max, negate=True).then_inc(rmax_ready, 1)
                dve.wait_ge(rexp_ready, b + 1)
                step.did(dve.tensor_reduce(rsum[:, :], rexp[:, :, :], AX.X, ALU.add))
                step.order()
                step.did(dve.reciprocal(rrec[:, :], rsum[:, :]))
                step.order()
                step.did(dve.tensor_tensor(rp[:, :, 0:EXPERTS], rexp[:, :, :],
                                           rrec[:, :].unsqueeze(2).broadcast_to([P, TPB, EXPERTS]), ALU.mult))
                step.order()
                step.alone()
                for t in range(TPB):
                    step.did(dve.max(rtop[:, t, :], rp[:, t, 0:EXPERTS]))
                step.order()
                step.did(dve.memset(rtop[:, :, TOPK:8], SENTINEL))
                step.order()
                step.alone()
                for t in range(TPB):
                    step.did(dve.match_replace(rq[:, t, :], rtop[:, t, :], rp[:, t, :], TAKEN))
                step.did(dve.tensor_reduce(rwsum[:, :], rtop[:, :, 0:TOPK], AX.X, ALU.add))
                step.order()
                step.did(dve.tensor_scalar(rsum[:, :], rwsum[:, :], 1e-20, None, ALU.add))
                here = sel[:, bass.ds(b * 2, 2), :]
                step.did(dve.tensor_scalar(here, rq[:, :, 0:EXPERTS], TAKEN, None, ALU.is_equal))
                step.order()
                step.did(dve.reciprocal(rwrec[:, :], rsum[:, :]))
                step.did(dve.tensor_tensor(rexp[:, :, :], rp[:, :, 0:EXPERTS], here, ALU.mult))
                step.order()
                dve.tensor_tensor(comb[:, bass.ds(b * 2, 2), :], rexp[:, :, :],
                                  rwrec[:, :].unsqueeze(2).broadcast_to([P, TPB, EXPERTS]), ALU.mult)\
                   .then_inc(sel_ready, 1)

            def iteration(b, first=False, last=False):
                if not last:
                    lo(xt[1], ps_xt, xt[0], xt_hi, b + 2, xt_lo)
                dve.wait_ge(sc_taken, b + 1)
                for r in range(4):
                    top_round(r)
                if not first:
                    residual(b - 1)
                    norm_stats(b - 1, stats2, mv2, ve2, ln2_var)
                for r in range(4, ROUNDS):
                    top_round(r)
                if not first:
                    ln2_apply(b - 1)
                masked_probs(b)
                if not last:
                    lo(qt[1], ps_qo, qt[0], q_hi, b + 2, q_lo)
                if not first:
                    lo(x2[1], ps_xt, x2[0], x2_hi, b, x2_lo)
                if not (isinstance(b, int) and b >= BATCH - 2):
                    ln1_stats(b + 2)
                lo(pt[1], ps_pt, pt[0], pt_hi, b + 1, pt_lo)
                if not (isinstance(b, int) and b >= BATCH - 2):
                    ln1_apply(b + 2)
                lo(ot[1], ps_qo, ot[0], o_hi, b + 1, o_lo)
                if not first:
                    router(b - 1)

            dve.memset(zeros, 0.0).then_inc(zeros_made, 1)
            step.did(dve.memset(rp[:, :, :], SENTINEL))
            step.did(dve.memset(delta[:, :], float(SLOT)))
            step.order()
            step.did(dve.memset(delta[:, 1:EXPERTS:SLOTS], float(SLOT * (1 - SLOTS))))
            ln1_stats(0)
            lo(wq[1], raw_q, wq[0], wqo_hi, 1, wqo_split)
            ln1_apply(0)
            lo(wo[1], raw_o, wo[0], wqo_hi, 2, wqo_split)
            lo(gw[1], raw_gw[:, :, :], gw[0], wqo_hi, 3, wqo_split)
            dve.wait_ge(coef_exp, 1)
            step.did(dve.tensor_scalar(cf[:, 2:3], cf[:, 0:1], 1.0, None, ALU.add))
            step.order()
            step.did(dve.reciprocal(cf[:, 3:4], cf[:, 2:3]))
            step.order()
            step.did(dve.tensor_scalar(cf[:, 4:5], cf[:, 3:4], -1.0, 1.0, ALU.mult, ALU.add))
            step.order()
            step.did(dve.tensor_tensor(cf[:, 5:6], cf[:, 4:5], scal[:, 1:2], ALU.mult))
            step.order()
            step.did(dve.scalar_tensor_tensor(out=cf[:, 6:7], in0=scal[:, 0:1], scalar=cf[:, 3:4], in1=cf[:, 5:6],
                                              op0=ALU.mult, op1=ALU.add))
            step.order()
            dve.tensor_scalar(coef, cf[:, 6:7], SCALE, cf[:, 1:2], ALU.mult, ALU.mult).then_inc(coef_ready, 1)
            lo(xt[1], ps_xt, xt[0], xt_hi, 1, xt_lo)
            ln1_stats(1)
            ln1_apply(1)
            lo(qt[1], ps_qo, qt[0], q_hi, 1, q_lo)
            iteration(0, first=True)
            iteration(1)
            with dve.Fori(2, BATCH - 2) as b:
                step.enter(b, 2, 49)
                iteration(b)
                step.leave(BATCH - 4)
            iteration(BATCH - 2)
            iteration(BATCH - 1, last=True)
            residual(BATCH - 1)
            norm_stats(BATCH - 1, stats2, mv2, ve2, ln2_var)
            ln2_apply(BATCH - 1)
            lo(x2[1], ps_xt, x2[0], x2_hi, BATCH, x2_lo)
            router(BATCH - 1)

            dve.wait_ge(sel_ready, BATCH)
            flat = sel[:, :, :].rearrange("p t e -> p (t e)")
            step.did(dve.tensor_tensor_scan(run[:, :, :].rearrange("p t e -> p (t e)"), flat, flat, 0.0,
                                            ALU.add, ALU.max))
            dve.wait_ge(consts_made, 5)
            dve.wait_ge(rank_mm, 2)
            step.did(dve.tensor_tensor(cmp_e[:, :, :], ps_tot.unsqueeze(2).broadcast_to([P, EXPERTS, EXPERTS]),
                                       blocks_m[:, :].unsqueeze(1).broadcast_to([P, EXPERTS, EXPERTS]), ALU.is_gt))
            step.order()
            step.did(dve.tensor_tensor(pick[:, :, :], run[:, :, :], six_t[:, :, :], ALU.subtract))
            step.did(dve.tensor_reduce(nblk[:, :], cmp_e[:, :, :], AX.X, ALU.add))
            step.order()
            step.did(dve.tensor_tensor(run[:, :, :], pick[:, :, :], sel[:, :, :], ALU.mult))
            step.did(dve.tensor_scalar(nblk1[:, :], nblk[:, :], 1.0, None, ALU.max))
            step.order()
            step.did(dve.tensor_tensor_scan(ends[:, :], nblk1[:, :], nblk1[:, :], 0.0, ALU.add, ALU.max))
            step.order()
            step.did(dve.tensor_tensor(starts[:, :], ends[:, :], nblk1[:, :], ALU.subtract))
            step.order()
            step.did(dve.scalar_tensor_tensor(out=posn[:, :, :], in0=starts[:, :].unsqueeze(1).broadcast_to([P, TILES, EXPERTS]),
                                              scalar=float(P), in1=ps_rank, op0=ALU.mult, op1=ALU.add))
            step.did(dve.memset(ends[:, EXPERTS - 1:EXPERTS], float(ROUTED)))
            for k in range(TOPK):
                step.order()
                step.did(dve.scalar_tensor_tensor(out=pick[:, :, :], in0=run[:, :, :], scalar=float(k + 1), in1=posn[:, :, :],
                                                  op0=ALU.is_equal, op1=ALU.mult))
                step.order()
                with nc.allow_low_precision(reason="row numbers are exact integers below 2^24"):
                    ins = dve.tensor_reduce(idx[:, :, k], pick[:, :, :], AX.X, ALU.add)
                if k == TOPK - 1:
                    ins.then_inc(idx_ready, 1)
                    dve.wait_ge(idx_ready, 1)
                else:
                    step.did(ins)
            step.order()
            dve.wait_ge(zero_filled, 16 * (ROUTED // 8))
            row = cmp_block[0:1, :, :]
            step.did(dve.tensor_tensor(row, ends[0:1, :].unsqueeze(1).broadcast_to([1, ROUTED, EXPERTS]),
                                       blk_i[0:1, :].unsqueeze(2).broadcast_to([1, ROUTED, EXPERTS]), ALU.is_le))
            step.order()
            step.did(dve.tensor_reduce(seq_f[0:1, :], row, AX.X, ALU.add))
            step.order()
            step.did(dve.tensor_tensor(row, row, delta[0:1, :].unsqueeze(1).broadcast_to([1, ROUTED, EXPERTS]), ALU.mult))
            step.order()
            step.did(dve.tensor_reduce(slot_f[0:1, :], row, AX.X, ALU.add))
            step.did(dve.memset(slot_tab[:, 0:TILES], 0))
            step.did(dve.memset(ready_tab[:, 0:TILES], 1))
            step.did(dve.memset(slot_tab[:, TILES + ROUTED:BLOCKS], (SETS - 1) % SLOTS * SLOT))
            step.did(dve.memset(ready_tab[:, TILES + ROUTED:BLOCKS], SETS))
            step.order()
            step.did(dve.tensor_scalar(slot_tab[:, TILES:TILES + ROUTED], slot_f[0:1, :], float(SLOT), None, ALU.add))
            step.did(dve.tensor_scalar(ready_tab[:, TILES:TILES + ROUTED], seq_f[0:1, :], 2.0, None, ALU.add))
            step.did(dve.tensor_scalar(end_tab[:, :], ends[0:1, :], float(TILES), None, ALU.add))
            step.order()
            dve.memset(hid[:, INNER:HPAD], 0.0).then_inc(tables_ready, 1)
            dve.wait_ge(tables_ready, 1)

            def tokens_lo(n, j):
                lo(bx[j % 2][1], ps_bx, bx[j % 2][0], bx_hi, n + 1, bx_lo)

            def hidden_lo(n):
                lo(htl, ps_ht, hth, ht_hi, n + 1, ht_lo)

            def hidden(n):
                dve.wait_ge(silu_ready, n + 1)
                if not (isinstance(n, int) and n == 0):
                    dve.wait_ge(ht_mm, n)
                dve.tensor_tensor(hid[:, 0:INNER], silu, ps_u, ALU.mult).then_inc(hid_ready, 1)

            def add_tile(n, j, t):
                dve.wait_ge(down_mm, n + 1)
                dve.tensor_tensor(acc[:, t, :], ps_y[j % 2], acc[:, t, :], ALU.add).then_inc(y_taken, 1)

            def take_y(n, j, stores):
                dve.wait_ge(down_mm, n + 1)
                if stores is not None:
                    dve.wait_ge(y_stored[j % 2], stores)
                dve.tensor_copy(ys[j % 2], ps_y[j % 2]).then_inc(y_taken, 1)

            def add_rows(n, t, j):
                for k in range(TOPK):
                    r = (j * TOPK + k) % RING
                    uses = UNROLL * TOPK // RING
                    nth = (j * TOPK + k) // RING + 1
                    dve.wait_ge(gathered[r], (t - j) * (16 * uses // UNROLL) + 16 * nth)
                    if k == 0:
                        dve.wait_ge(y_taken, n + 1)
                    else:
                        dve.wait_ge(row_added, t * TOPK + k)
                    dve.scalar_tensor_tensor(out=acc[:, t, :], in0=ring[r], scalar=wgt[:, t, k:k + 1],
                                             in1=acc[:, t, :], op0=ALU.mult, op1=ALU.add).then_inc(row_added, 1)

            def front(n, j, first=False, last=False):
                if not last:
                    tokens_lo(n + 1, j + 1)
                if not first:
                    hidden_lo(n - 1)
                hidden(n)

            tokens_lo(0, 0)
            front(0, 0, first=True)
            for k in range(TOPK):
                step.did(dve.scalar_tensor_tensor(out=pick[:, :, :], in0=run[:, :, :], scalar=float(k + 1), in1=comb[:, :, :],
                                                  op0=ALU.is_equal, op1=ALU.mult))
                step.order()
                step.did(dve.tensor_reduce(wgt[:, :, k], pick[:, :, :], AX.X, ALU.add))
                step.order()
            for j in range(1, UNROLL):
                front(j, j)
                add_tile(j - 1, j - 1, j - 1)
            with dve.Fori(1, TILES // UNROLL) as g:
                for j in range(UNROLL):
                    n = g * UNROLL + j
                    front(n, j)
                    add_tile(n - 1, j + UNROLL - 1, n - 1)
            first = TILES // UNROLL
            for j in range(UNROLL):
                n = first * UNROLL + j
                front(n, j)
                if j == 0:
                    add_tile(n - 1, UNROLL - 1, n - 1)
                else:
                    take_y(n - 1, j - 1, None if j < 3 else 16)
            with dve.Fori(first + 1, (TILES + ROUTED) // UNROLL) as g:
                for j in range(UNROLL):
                    n = g * UNROLL + j
                    front(n, j)
                    m = (j - 1) % UNROLL
                    done = (g - first) * 2 + (m // 2 if j else m // 2 - 2)
                    take_y(n - 1, m, done * 16)
            n = TILES + ROUTED
            front(n, 0)
            take_y(n - 1, UNROLL - 1, (ROUTED // 2 - 1) * 16)
            for j in range(1, UNROLL):
                front(n + j, j)
                add_tile(n + j - 1, j - 1, j - 1)
                add_rows(n + j - 1, j - 1, j - 1)
            with dve.Fori(1, TILES // UNROLL - 1) as g:
                for j in range(UNROLL):
                    t = g * UNROLL + j
                    m = (j - 1) % UNROLL
                    front(t + n, j)
                    add_tile(t + (n - 1), m, t - 1)
                    add_rows(t + (n - 1), t - 1, m)
            for j in range(UNROLL):
                t = TILES - UNROLL + j
                m = (j - 1) % UNROLL
                front(n + t, j, last=j == UNROLL - 1)
                add_tile(n + t - 1, m, t - 1)
                add_rows(n + t - 1, t - 1, m)
            hidden_lo(BLOCKS - 1)
            add_tile(BLOCKS - 1, UNROLL - 1, TILES - 1)
            add_rows(BLOCKS - 1, TILES - 1, UNROLL - 1)

        @block.gpsimd
        def _(pool):
            step = Steps(pool, pool_step)

            def split_ctx_t(b):
                pool.wait_ge(ctx_t_in, b * 16 + 16)
                if not (isinstance(b, int) and b == 0):
                    pool.wait_ge(sc_mm, b)
                step.alone()
                pool.tensor_copy(ct[0], raw_ct).then_inc(ct_split, 1)
                pool.wait_ge(ct_split, b * 2 + 1)
                pool.tensor_tensor(ct[1], raw_ct, f32(ct[0]), ALU.subtract).then_inc(ct_split, 1)

            def split_ctx_n(b):
                pool.wait_ge(ctx_n_in, b * 16 + 16)
                if not (isinstance(b, int) and b == 0):
                    pool.wait_ge(o_mm, b)
                step.alone()
                pool.tensor_copy(cn[0], raw_cn).then_inc(cn_split, 1)
                pool.wait_ge(cn_split, b * 2 + 1)
                pool.tensor_tensor(cn[1], raw_cn, f32(cn[0]), ALU.subtract).then_inc(cn_split, 1)

            def root(b, var, ve, rstd, done):
                pool.wait_ge(var, b + 1)
                pool.tensor_tensor(rstd[:, :], ve[:, :], neghalf[:, :], ALU.pow).then_inc(done, 1)

            def iteration(b, first=False, last=False):
                if not last:
                    split_ctx_t(b + 1)
                if not first:
                    root(b - 1, ln2_var, ve2, rstd2, ln2_rstd)
                if not (isinstance(b, int) and b >= BATCH - 2):
                    root(b + 2, ln1_var, ve1, rstd1, ln1_rstd)
                if not last:
                    split_ctx_n(b + 1)

            step.did(pool.memset(ident[:, :], 0.0))
            step.did(pool.memset(upper[:, :], 1.0))
            step.did(pool.memset(neghalf[:, :], -0.5))
            step.order()
            pool.affine_select(out=ident[:, :], in_=ident[:, :], compare_op=ALU.not_equal, fill=1.0,
                               base=0, pattern=[[-1, P]], channel_multiplier=1).then_inc(consts_made, 1)
            pool.affine_select(out=upper[:, :], in_=upper[:, :], compare_op=ALU.is_gt, fill=0.0,
                               base=0, pattern=[[1, P]], channel_multiplier=-1).then_inc(consts_made, 1)
            root(0, ln1_var, ve1, rstd1, ln1_rstd)
            pool.memset(ones[:, :], 1.0)
            pool.iota(blk_i[:, :], [[1, ROUTED]], base=0, channel_multiplier=0, allow_small_or_imprecise_dtypes=True)
            pool.iota(blocks_m[:, :], [[P, EXPERTS]], base=0, channel_multiplier=0, allow_small_or_imprecise_dtypes=True)\
                .then_inc(consts_made, 1)
            pool.iota(six_t[:, :, :], [[TOPK, TILES], [0, EXPERTS]], base=0, channel_multiplier=0,
                      allow_small_or_imprecise_dtypes=True).then_inc(consts_made, 1)
            split_ctx_t(0)
            pool.memset(idx_now[0][:, :], 0).then_inc(consts_made, 1)
            split_ctx_n(0)
            root(1, ln1_var, ve1, rstd1, ln1_rstd)
            iteration(0, first=True)
            iteration(1)
            with pool.Fori(2, BATCH - 2) as b:
                iteration(b)
            iteration(BATCH - 2)
            iteration(BATCH - 1, last=True)

            w13_v = w13.rearrange("(e p) n -> p e n", p=P)
            w2_v = w2.rearrange("(e r) n -> r e n", r=INNER)
            sw13_v = sw13.rearrange("(e p) n -> p e n", p=P)
            sw2_v = sw2.rearrange("(e r) n -> r e n", r=INNER)
            rest = INNER - (HC - 1) * P

            def load_weights(up, dn, e):
                pool.dma_start(raw[:, 0:W13], up[:, e, :]).then_inc(w_in, 16)
                for c in range(HC):
                    rows = P if c < HC - 1 else rest
                    pool.dma_start(raw[0:rows, W13 + c * D:W13 + (c + 1) * D],
                                   dn[c * P:c * P + rows, e, :]).then_inc(w_in, 16)

            def split_weights(n):
                at = (n % SLOTS if isinstance(n, int) else 0) * SLOT
                split_into(n, at)

            def split_into(n, at):
                pool.wait_ge(w_in, n * 64 + 64)
                step.alone()
                step.did(pool.tensor_copy(slots[:, at:at + WSET], raw[:, :]))
                step.order()
                pool.tensor_tensor(slots[:, at + WSET:at + SLOT], raw[:, :], f32(slots[:, at:at + WSET]), ALU.subtract)\
                    .then_inc(w_ready, 1)
                pool.wait_ge(w_ready, n + 1)

            pool.wait_ge(cn_split, 2 * BATCH)
            pool.wait_ge(ln2_rstd, BATCH - 1)
            step.did(pool.memset(raw[rest:P, W13 + (HC - 1) * D:WSET], 0.0))
            step.order()
            load_weights(sw13_v, sw2_v, 0)
            root(BATCH - 1, ln2_var, ve2, rstd2, ln2_rstd)
            split_into(0, 0)
            load_weights(w13_v, w2_v, 0)
            pool.wait_ge(y_mm, TILES)
            split_into(1, SLOT)
            load_weights(w13_v, w2_v, 1)

            pool.wait_ge(idx_ready, 1)
            pool.wait_ge(zero_filled, 16 * (ROUTED // 8))
            def scatter(g, first=False):
                for j in range(UNROLL):
                    t = g * UNROLL + j
                    if not first:
                        pool.wait_ge(scattered[j], g * (16 * TOPK))
                    step.alone()
                    step.did(pool.tensor_copy(idx_now[j][:, :], idx[:, t, :]))
                    pool.wait_ge(xb_in[j], g * 16 + 16)
                    step.order()
                    step.alone()
                    for k in range(TOPK):
                        pool.indirect_dma_start(sorted_dram[:, :], bass.IndirectOffsetOnAxis(idx_now[j][:, k:k + 1], 0),
                                                xb[j], None).then_inc(scattered[j], 16)
            scatter(0, first=True)
            with pool.Fori(1, TILES // UNROLL) as g:
                step.enter(g, 1, UNROLL)
                scatter(g)
                step.leave(TILES // UNROLL - 1)
            split_into(2, 2 * SLOT)
            load_weights(w13_v, w2_v, 2)
            pool.wait_ge(down_mm, TILES)
            split_into(3, 0)
            load_weights(w13_v, w2_v, 3)
            pool.wait_ge(tables_ready, 1)
            with pool.Fori(0, 4) as m:
                step.enter(m, 0, SLOTS)
                for s in range(SLOTS):
                    n = m * SLOTS + (4 + s)
                    done = pool.value_load(end_tab[0:1, bass.ds(m * SLOTS + s, 1)], min_val=TILES + 1, max_val=TILES + ROUTED)
                    pool.wait_ge(down_mm, done)
                    split_into(n, (4 + s) % SLOTS * SLOT)
                    load_weights(w13_v, w2_v, n)
                step.leave(4)
            for n in (16, 17):
                done = pool.value_load(end_tab[0:1, n - 4:n - 3], min_val=TILES + 1, max_val=TILES + ROUTED)
                pool.wait_ge(down_mm, done)
                split_into(n, n % SLOTS * SLOT)
                if n == 16:
                    load_weights(sw13_v, sw2_v, 1)

            for j in range(2):
                pool.wait_ge(y_stored[j], 16 * ROUTED // 2)
            def gather(g, first=False):
                for j in range(UNROLL):
                    t = g * UNROLL + j
                    step.alone()
                    step.did(pool.tensor_copy(idx_now[j][:, :], idx[:, t, :]))
                    step.order()
                    for k in range(TOPK):
                        i = j * TOPK + k
                        if not (first and i < RING):
                            pool.wait_ge(row_added, g * (UNROLL * TOPK) + (i - RING + 1))
                        step.alone()
                        pool.indirect_dma_start(ring[i % RING], None, y_dram[:, :],
                                                bass.IndirectOffsetOnAxis(idx_now[j][:, k:k + 1], 0))\
                            .then_inc(gathered[i % RING], 16)
            gather(0, first=True)
            with pool.Fori(1, TILES // UNROLL) as g:
                step.enter(g, 1, UNROLL)
                gather(g)
                step.leave(TILES // UNROLL - 1)


def kernel(**inputs):
    import numpy as _np
    import concourse.bacc as _bacc
    from concourse import mybir as _mybir
    from concourse.bass_utils import run_bass_kernel_spmd as _run

    def chunks(a, last):
        lead = a.shape[:-2]
        a = a.reshape(-1, KC, P, last).transpose(0, 2, 1, 3)
        return _np.ascontiguousarray(a).reshape(-1, KC * last)

    g = {k: _np.asarray(v) for k, v in inputs.items()}
    ctx = g["ctx_2048"]
    sw13 = g["L0_ffn_sw13"].reshape(2, 2, INNER, D).transpose(1, 3, 0, 2)
    arrays = {
        "x": g["x"].reshape(TOKENS, D),
        "ctx_n": ctx.reshape(TOKENS, D),
        "ctx_t": chunks(ctx.transpose(0, 2, 1), SEQ),
        "wq_t": chunks(g["L0_xattn_W_qkv"][:D].T[None], D),
        "wo_t": chunks(g["L0_xattn_W_o"].T[None], D),
        "beta_q": g["L0_xattn_beta_q"].reshape(1, 1),
        "beta_k": g["L0_xattn_beta_k"].reshape(1, 1),
        "gate": g["L0_xattn_gate"].reshape(1, 1),
        "log_tau": g["L0_xattn_log_tau"].reshape(1, 1),
        "gate_w_t": g["L0_ffn_gate_w"].T,
        "w13": chunks(g["L0_ffn_w13"].transpose(0, 2, 1), 2 * INNER),
        "w2": g["L0_ffn_w2"].transpose(0, 2, 1).reshape(EXPERTS * INNER, D),
        "sw13": chunks(sw13.reshape(2, D, 2 * INNER), 2 * INNER),
        "sw2": g["L0_ffn_sw2"].T,
    }
    arrays = {k: _np.ascontiguousarray(v) for k, v in arrays.items()}
    nc = _bacc.Bacc("TRN2", target_bir_lowering=False, num_devices=1)
    args = [nc.dram_tensor(k, v.shape, _mybir.dt.from_np(v.dtype), kind="ExternalInput").ap()
            for k, v in arrays.items()]
    args.append(nc.dram_tensor("out", (TOKENS, D), _mybir.dt.float32, kind="ExternalOutput").ap())
    xattn_moe(nc, *args)
    r = _run(nc, [arrays], core_ids=[0])
    return r.results[0]["out"].reshape(BATCH, SEQ, D)
```

```python
from contextlib import ExitStack

import concourse.bass as bass
from concourse import mybir

F32 = mybir.dt.float32
F32R = mybir.dt.float32r
BF16 = mybir.dt.bfloat16
I32 = mybir.dt.int32
ALU = mybir.AluOpType
ACT = mybir.ActivationFunctionType
AX = mybir.AxisListType

P = 128
BATCH, SEQ, D = 8, 256, 512
KEEP = 54
TOKENS = BATCH * SEQ
TILES = TOKENS // P
TPB = SEQ // P
KC = D // P
NC = SEQ // P
EXPERTS, TOPK = 16, 6
INNER = 352
HC = 3
HPAD = HC * P
ROUTED = TOKENS * TOPK // P + EXPERTS
BLOCKS = TILES + ROUTED + TILES
SETS = EXPERTS + 2
W13 = KC * 2 * INNER
WSET = W13 + HC * D
SLOT = 2 * WSET
HALF_A = WSET - 2 * INNER - HC * D
SLOTS = 3
STEADY = 2
UNROLL = 4
FIRST_ROUTED = TILES // UNROLL
FIRST_SPARE = (TILES + ROUTED - EXPERTS) // UNROLL
END_ROUTED = (TILES + ROUTED) // UNROLL
READY = 3
RING = 12
EPS = 1e-5
SCALE = float(D) ** -0.5
ROUNDS = -(-KEEP // 8)
DVE_STEPS, ROUTER_STEPS = 36, 13
LOWEST = -3.0e38
SENTINEL, TAKEN = -1.0, -2.0


class Steps:

    def __init__(self, eng, sem):
        self.eng, self.sem, self.base, self.n = eng, sem, 0, 0
        
    def did(self, instruction):
        instruction.then_inc(self.sem, 1)
        self.n += 1

    def order(self):
        self.eng.wait_ge(self.sem, self.base + self.n)

    def order_before_last(self):
        self.eng.wait_ge(self.sem, self.base + (self.n - 1))

    def alone(self):
        self.eng.nop(nofuse=True)

    def enter(self, i, first, per):
        self.before, self.per, self.base, self.n = self.n, per, i * per + (self.n - first * per), 0

    def leave(self, count):
        assert self.n == self.per, f"{self.sem}: {self.n} steps in an iteration, not {self.per}"
        self.base, self.n = 0, self.before + count * self.per


def xattn_moe(nc, x, ctx_n, ctx_t, wq_t, wo_t, beta_q, beta_k, gate, log_tau, gate_w_t,
              w13, w2, sw13, sw2, out):
    with ExitStack() as stack:
        def sb(name, shape, dt=F32):
            return stack.enter_context(nc.sbuf_tensor(name, shape, dt))

        def sem(name):
            return stack.enter_context(nc.semaphore(name))

        xn2_dram = nc.dram_tensor("xn2_dram", [TOKENS, D], F32, kind="Internal")
        sorted_dram = nc.dram_tensor("sorted_dram", [ROUTED * P, D], F32, kind="Internal")
        y_dram = nc.dram_tensor("y_dram", [ROUTED * P, D], F32, kind="Internal")

        acc = sb("acc", [P, TILES, D])
        raw = sb("raw", [P, WSET])
        slots = sb("slots", [P, SLOTS * SLOT], F32R)
        tail = sb("tail", [P, 3072], F32R)
        x2 = sb("x2", [P, KC, SEQ])
        arena = sb("arena", [P, 4096])
        tab = sb("tab", [P, 1792])

        def carve(tensor, at, *dims):
            n = 1
            for d in dims:
                n *= d
            ap = tensor[:, at:at + n]
            names = "abc"[:len(dims)]
            if len(dims) > 1:
                ap = ap.rearrange(f"p ({' '.join(names)}) -> p {' '.join(names)}",
                                  **dict(zip(names[1:], dims[1:])))
            return ap, at + n

        at = SLOT
        pairs = {}
        for name, dims in (("wq", (KC, D)), ("wo", (KC, D)), ("xt", (KC, SEQ)), ("cn", (NC, D)),
                           ("ct", (KC, SEQ)), ("qt", (KC, SEQ))):
            hi, at = carve(slots, at, *dims)
            lo, at = carve(slots, at, *dims)
            pairs[name] = (hi, lo)
        assert at <= SLOTS * SLOT
        at = 0
        for name, dims in (("pt", (NC, SEQ)), ("ot", (KC, SEQ))):
            hi, at = carve(tail, at, *dims)
            lo, at = carve(tail, at, *dims)
            pairs[name] = (hi, lo)
        wq, wo, xt, cn, ct, qt = (pairs[k] for k in ("wq", "wo", "xt", "cn", "ct", "qt"))
        pt, ot = (pairs[k] for k in ("pt", "ot"))
        xn, at = carve(arena, 0, TPB, D)
        xn2, at = carve(arena, at, TPB, D)
        sc, at = carve(arena, at, TPB, SEQ)
        left, at = carve(arena, at, TPB, SEQ)
        shifted, at = carve(arena, at, TPB, SEQ)
        probs, at = carve(arena, at, TPB, SEQ)
        raw_q, at = carve(raw, 0, KC, D)
        raw_o, at = carve(raw, at, KC, D)
        raw_cn, at = carve(raw, 0, NC, D)
        raw_ct, at = carve(raw, at, KC, SEQ)
        stage = raw[:, at:WSET]
        assert max(HALF_A, WSET - HALF_A) <= WSET - at
        bx = [None, None]
        at = 0
        for j in range(2):
            hi, at = carve(tail, at, KC, P)
            lo, at = carve(tail, at, KC, P)
            bx[j] = (hi, lo)
        hth, at = carve(tail, at, HC, P)
        htl, at = carve(tail, at, HC, P)
        xb = [None] * UNROLL
        at = 0
        for j in range(UNROLL):
            xb[j], at = carve(arena, at, D)
        ys = [None] * 2
        for j in range(2):
            ys[j], at = carve(arena, at, D)
        hid, at = carve(arena, at, HPAD)
        silu, at = carve(arena, at, INNER)
        assert at <= 4096
        zeros = tab[:, 0:D]
        cmp_block = tab[:, 0:ROUTED * EXPERTS].rearrange("p (i e) -> p i e", e=EXPERTS)
        ring = [raw[:, r * D:(r + 1) * D] for r in range(WSET // D)]
        ring += [x2[:, c:c + D // SEQ, :].rearrange("p c n -> p (c n)") for c in range(0, KC, D // SEQ)]
        ring += [tab[:, r * D:(r + 1) * D] for r in range(RING - len(ring))]
        ident = sb("ident", [P, P])
        upper = sb("upper", [P, P], BF16)
        ones = sb("ones", [P, P], BF16)
        raw_gw = sb("raw_gw", [P, KC, EXPERTS])
        scal = sb("scal", [P, 4])
        cf = sb("cf", [P, 8])
        coef = cf[:, 7:8]
        neghalf = sb("neghalf", [P, TPB])
        stats1 = sb("stats1", [P, TPB, 6])
        stats2 = sb("stats2", [P, TPB, 6])
        mv1 = sb("mv1", [P, TPB, 2])
        mv2 = sb("mv2", [P, TPB, 2])
        ve1 = sb("ve1", [P, TPB])
        ve2 = sb("ve2", [P, TPB])
        negm1 = sb("negm1", [P, TPB])
        negm2 = sb("negm2", [P, TPB])
        rstd1 = sb("rstd1", [P, TPB])
        rstd2 = sb("rstd2", [P, TPB])
        shift1 = sb("shift1", [P, TPB])
        shift2 = sb("shift2", [P, TPB])
        top8 = sb("top8", [P, TPB, 8])
        negmax = sb("negmax", [P, TPB])
        thr = sb("thr", [P, TPB])
        psums = sb("psums", [P, TPB])
        rinv = sb("rinv", [P, TILES])
        rneg = sb("rneg", [P, TPB])
        rexp = sb("rexp", [P, TPB, EXPERTS])
        rsum = sb("rsum", [P, TPB])
        rrec = sb("rrec", [P, TPB])
        rp = sb("rp", [P, TPB, EXPERTS + 2])
        rq = sb("rq", [P, TPB, EXPERTS + 2])
        rtop = sb("rtop", [P, TPB, 8])
        rwsum = sb("rwsum", [P, TPB])
        rwrec = sb("rwrec", [P, TPB])
        sel = sb("sel", [P, TILES, EXPERTS], BF16)
        comb = sb("comb", [P, TILES, EXPERTS])
        run = sb("run", [P, TILES, EXPERTS])
        six_t = sb("six_t", [P, TILES, EXPERTS])
        pick = sb("pick", [P, TILES, EXPERTS])
        picks = [pick[:, :, :]] + [ys[0][:, s:s + TILES * EXPERTS].rearrange("p (t e) -> p t e", e=EXPERTS)
                                  for s in (0, TILES * EXPERTS)]
        blocks_m = sb("blocks_m", [P, EXPERTS])
        nblk = sb("nblk", [P, EXPERTS])
        nblk1 = sb("nblk1", [P, EXPERTS])
        ends = sb("ends", [P, EXPERTS])
        starts = sb("starts", [P, EXPERTS])
        posn = sb("posn", [P, TILES, EXPERTS])
        cmp_e = posn
        delta = sb("delta", [P, EXPERTS])
        blk_i = sb("blk_i", [P, ROUTED])
        seq_f = sb("seq_f", [P, ROUTED])
        slot_f = sb("slot_f", [P, ROUTED])
        idx = sb("idx", [P, TILES, TOPK], I32)
        wgt = sb("wgt", [P, TILES, TOPK])
        idx_now = [sb(f"idx_now{h}", [P, 2, TOPK], I32) for h in range(UNROLL // 2)]
        slot_tab = sb("slot_tab", [1, BLOCKS], I32)
        ready_tab = sb("ready_tab", [1, BLOCKS], I32)
        used_end = sb("used_end", [1, 1], I32)
        end_tab = sb("end_tab", [1, EXPERTS], I32)

        ps = stack.enter_context(nc.psum_tensor("ps", [P, 8, 512], F32))
        ps_xt = ps[:, 0:2, :].rearrange("p a (b n) -> p (a b) n", n=SEQ)
        ps_x2 = ps[:, 6:8, :].rearrange("p a (b n) -> p (a b) n", n=SEQ)
        ps_qo = ps[:, 2:4, :].rearrange("p a (b n) -> p (a b) n", n=SEQ)
        ps_sc = ps[:, 4, :].rearrange("p (t n) -> p t n", n=SEQ)
        ps_pt = ps[:, 5, :].rearrange("p (c n) -> p c n", n=SEQ)
        ps_lg = ps[:, 5, 0:TPB * EXPERTS].rearrange("p (t e) -> p t e", e=EXPERTS)
        ps_y = [ps[:, 6, :], ps[:, 7, :]]
        ps_rank = ps[:, 4, 0:TILES * EXPERTS].rearrange("p (t e) -> p t e", e=EXPERTS)
        ps_tot = ps[:, 5, 0:EXPERTS]
        ps_bx = ps[:, 0, :].rearrange("p (c n) -> p c n", n=P)
        ps_ht = ps[:, 1, 0:HPAD].rearrange("p (c n) -> p c n", n=P)
        ps_g = ps[:, 2, 0:INNER]
        ps_u = ps[:, 3, 0:INNER]

        x_in = [sem("x_in0"), sem("x_in1"), sem("x_in2"), sem("x_in_rest")]
        wq_in = sem("wq_in")
        wo_in = sem("wo_in")
        small_in = sem("small_in")
        ctx_t_in = sem("ctx_t_in")
        ctx_n_in = sem("ctx_n_in")
        zeros_made = sem("zeros_made")
        zero_filled = sem("zero_filled")
        consts_made = sem("consts_made")
        pool_step = sem("pool_step")
        router_step = sem("router_step")
        dve_step = sem("dve_step")
        act_step = sem("act_step")
        wqo_hi = sem("wqo_hi")
        wqo_split = sem("wqo_split")
        coef_exp = sem("coef_exp")
        coef_ready = sem("coef_ready")
        ln1_var = sem("ln1_var")
        ln2_var = sem("ln2_var")
        ln1_rstd = sem("ln1_rstd")
        ln2_rstd = sem("ln2_rstd")
        xn_ready = sem("xn_ready")
        xt_mm = sem("xt_mm")
        xt_hi = sem("xt_hi")
        xt_lo = sem("xt_lo")
        q_mm = sem("q_mm")
        q_hi = sem("q_hi")
        q_lo = sem("q_lo")
        ct_split = sem("ct_split")
        cn_split = sem("cn_split")
        sc_mm = sem("sc_mm")
        sc_taken = sem("sc_taken")
        sc_free = sem("sc_free")
        max_ready = sem("max_ready")
        exp_ready = sem("exp_ready")
        probs_ready = sem("probs_ready")
        pt_mm = sem("pt_mm")
        pt_hi = sem("pt_hi")
        pt_lo = sem("pt_lo")
        o_mm = sem("o_mm")
        o_hi = sem("o_hi")
        o_lo = sem("o_lo")
        y_mm = sem("y_mm")
        x1_ready = sem("x1_ready")
        xn2_ready = sem("xn2_ready")
        xn2_stored = sem("xn2_stored")
        x2_mm = sem("x2_mm")
        x2_taken = sem("x2_taken")
        lg_mm = sem("lg_mm")
        rmax_ready = sem("rmax_ready")
        rexp_ready = sem("rexp_ready")
        sel_ready = sem("sel_ready")
        rank_mm = sem("rank_mm")
        idx_ready = sem("idx_ready")
        tables_ready = sem("tables_ready")
        set0_in = [sem("set0a_in"), sem("set0b_in")]
        set1_in = sem("set1_in")
        set2_in = sem("set2_in")
        pads_zeroed = sem("pads_zeroed")
        first_hi = sem("first_hi")
        first_lo = sem("first_lo")
        next_hi = sem("next_hi")
        w_in = sem("w_in")
        w_ready = sem("w_ready")
        xb_in = [sem(f"xb_in{j}") for j in range(UNROLL)]
        scattered = [sem(f"scattered{j}") for j in range(UNROLL)]
        bx_mm = sem("bx_mm")
        bx_hi = sem("bx_hi")
        bx_lo = sem("bx_lo")
        gu_mm = sem("gu_mm")
        silu_ready = sem("silu_ready")
        hid_ready = sem("hid_ready")
        ht_mm = sem("ht_mm")
        ht_hi = sem("ht_hi")
        ht_lo = sem("ht_lo")
        down_mm = sem("down_mm")
        y_taken = sem("y_taken")
        y_stored = [sem(f"y_stored{j}") for j in range(2)]
        gathered = [sem(f"gathered{r}") for r in range(RING)]
        row_added = sem("row_added")
        out_stored = sem("out_stored")

        def split_piece(n, piece):
            if n == 0:
                at, size = piece * HALF_A, HALF_A if piece == 0 else WSET - HALF_A
                src = stage[:, 0:size]
            else:
                size = WSET // 4
                at = piece * size
                src = raw[:, at:at + size]
            at += n * SLOT
            return src, slots[:, at:at + size], slots[:, at + WSET:at + WSET + size]

        block = stack.enter_context(nc.Block())

        def parts3(a, b):
            return ((a[0], b[0]), (a[0], b[1]), (a[1], b[0]))

        def f32(ap):
            return ap.bitcast(F32)

        def load_used(eng):
            return eng.value_load(used_end[0:1, 0:1], min_val=0, max_val=EXPERTS) + (TILES + ROUTED - EXPERTS)

        def within(b):
            return not isinstance(b, int) or 0 <= b < BATCH

        ctx_t_v = ctx_t.rearrange("(b p) n -> b p n", p=P)
        ctx_n_v = ctx_n.rearrange("(b c p) n -> p b c n", c=NC, p=P)
        xn2_v = xn2_dram[:, :].rearrange("(t p) n -> p t n", p=P)
        sorted_v = sorted_dram[:, :].rearrange("(i p) n -> p i n", p=P)
        y_v = y_dram[:, :].rearrange("(i p) n -> p i n", p=P)
        out_v = out.rearrange("(t p) n -> p t n", p=P)
        x_v = x.rearrange("(t p) n -> p t n", p=P)
        w13_v = w13.rearrange("(e p) n -> p e n", p=P)
        w2_v = w2.rearrange("(e r) n -> r e n", r=INNER)
        sw13_v = sw13.rearrange("(e p) n -> p e n", p=P)
        sw2_v = sw2.rearrange("(e r) n -> r e n", r=INNER)
        rest = INNER - (HC - 1) * P

        @block.sync
        def _(sp):
            def load_ctx_t(b):
                sp.dma_start(raw_ct.rearrange("p c n -> p (c n)"), ctx_t_v[b, :, :] if isinstance(b, int)
                             else ctx_t_v[bass.ds(b, 1), :, :].rearrange("o p n -> p (o n)")).then_inc(ctx_t_in, 16)

            def load_ctx_n(b):
                sp.dma_start(raw_cn, ctx_n_v[:, b, :, :]).then_inc(ctx_n_in, 16)

            def store_xn2(b):
                sp.wait_ge(xn2_ready, 2 * b + 2)
                sp.dma_start(xn2_v[:, bass.ds(b * 2, 2), :], xn2).then_inc(xn2_stored, 16)

            sp.dma_start(acc[:, 0:2, :], x_v[:, 0:2, :]).then_inc(x_in[0], 16)
            sp.dma_start(raw_q.rearrange("p c n -> p (c n)"), wq_t).then_inc(wq_in, 16)
            for s, src in enumerate((beta_q, beta_k, gate, log_tau)):
                sp.dma_start(scal[:, s:s + 1], src[0, :].partition_broadcast(P)).then_inc(small_in, 16)
            sp.dma_start(raw_gw[:, :, :], gate_w_t.rearrange("(c p) e -> p c e", p=P)).then_inc(small_in, 16)
            sp.dma_start(acc[:, 2:4, :], x_v[:, 2:4, :]).then_inc(x_in[1], 16)
            sp.dma_start(raw_o.rearrange("p c n -> p (c n)"), wo_t).then_inc(wo_in, 16)
            sp.wait_ge(wqo_split, 1)
            load_ctx_t(0)
            load_ctx_n(0)
            for b in range(2, BATCH):
                sp.dma_start(acc[:, 2 * b:2 * b + 2, :], x_v[:, 2 * b:2 * b + 2, :]).then_inc(x_in[min(b, 3)], 16)

            def iteration(i):
                if within(i - 2):
                    store_xn2(i - 2)
                if 1 <= i + 3 < BATCH if isinstance(i, int) else True:
                    sp.wait_ge(ct_split, i * 2 + 6)
                    load_ctx_t(i + 3)
                if 1 <= i + 1 < BATCH if isinstance(i, int) else True:
                    sp.wait_ge(cn_split, i * 2 + 2)
                    load_ctx_n(i + 1)
                if 0 <= i + 1 < ROUTED // 16 if isinstance(i, int) else True:
                    for half in range(2):
                        sp.dma_start(sorted_v[:, bass.ds(i * 16 + (half * 8 + 16), 8), :],
                                     zeros.unsqueeze(1).broadcast_to([P, 8, D])).then_inc(zero_filled, 16)

            def load_down(at, dn, e, done):
                for c in range(HC):
                    rows = P if c < HC - 1 else rest
                    sp.dma_start(at[0:rows, c * D:(c + 1) * D], dn[c * P:c * P + rows, e, :]).then_inc(done, 16)

            sp.wait_ge(zeros_made, 1)
            for i in range(-2, STEADY):
                iteration(i)
            sp.wait_ge(wqo_split, 2)
            sp.dma_start(stage[:, 0:HALF_A], sw13_v[:, 0, 0:HALF_A]).then_inc(set0_in[0], 16)
            with sp.Fori(STEADY, BATCH - 3) as i:
                iteration(i)
            iteration(BATCH - 3)
            iteration(BATCH - 2)
            sp.wait_ge(first_lo, 1)
            sp.wait_ge(pads_zeroed, 1)
            sp.dma_start(stage[:, 0:W13 - HALF_A], sw13_v[:, 0, HALF_A:W13]).then_inc(set0_in[1], 16)
            load_down(stage[:, W13 - HALF_A:WSET - HALF_A], sw2_v, 0, set0_in[1])
            for half in range(2):
                sp.dma_start(y_v[:, ROUTED - EXPERTS + half * 8:ROUTED - EXPERTS + half * 8 + 8, :],
                             zeros.unsqueeze(1).broadcast_to([P, 8, D])).then_inc(zero_filled, 16)
            iteration(BATCH - 1)

            def load_block(n, src, tile, j, free=True):
                if free:
                    sp.wait_ge(bx_mm, n - UNROLL + 1)
                sp.dma_start(xb[j], src[:, tile, :]).then_inc(xb_in[j], 16)

            sp.wait_ge(xt_mm, BATCH)
            sp.wait_ge(xn2_stored, 16 * (BATCH - 2))
            load_block(0, xn2_v, 0, 0, free=False)
            load_block(1, xn2_v, 1, 1, free=False)
            iteration(BATCH)
            sp.wait_ge(pads_zeroed, 2)
            sp.dma_start(raw[:, 0:W13], w13_v[:, 0, :]).then_inc(set1_in, 16)
            load_down(raw[:, W13:WSET], w2_v, 0, set1_in)
            iteration(BATCH + 1)
            sp.wait_ge(xn2_stored, 16 * BATCH)
            sp.wait_ge(x2_mm, BATCH)
            load_block(2, xn2_v, 2, 2, free=False)
            load_block(3, xn2_v, 3, 3, free=False)
            with sp.Fori(1, TILES // UNROLL) as g:
                for j in range(UNROLL):
                    n = g * UNROLL + j
                    sp.wait_ge(scattered[j], g * (16 * TOPK))
                    sp.nop(nofuse=True)
                    load_block(n, xn2_v, n, j)
            sp.wait_ge(w_ready, 1 + READY)
            sp.dma_start(raw[:, 0:W13], w13_v[:, 1, :]).then_inc(set2_in, 16)
            load_down(raw[:, W13:WSET], w2_v, 1, set2_in)
            for j in range(UNROLL):
                sp.wait_ge(scattered[j], 16 * TOPK * TILES // UNROLL)
            with sp.Fori(FIRST_ROUTED, FIRST_ROUTED + 1) as g:
                for j in range(UNROLL):
                    load_block(g * UNROLL + j, sorted_v, g * UNROLL + (j - TILES), j)
            def load_and_store(g):
                for j in range(UNROLL):
                    n = g * UNROLL + j
                    load_block(n, sorted_v, n - TILES, j)
                    m = n - UNROLL
                    sp.wait_ge(y_taken, m + 1)
                    sp.dma_start(y_v[:, m - TILES, :], ys[j % 2]).then_inc(y_stored[j % 2], 16)

            with sp.Fori(FIRST_ROUTED + 1, FIRST_SPARE) as g:
                load_and_store(g)
            sp.wait_ge(tables_ready, 1)
            used = load_used(sp)
            with sp.Fori(FIRST_SPARE, END_ROUTED) as g:
                with sp.If(used > g * UNROLL):
                    load_and_store(g)
            for j in range(UNROLL):
                n, m = used + j, used + (j - UNROLL)
                load_block(n, xn2_v, j, j)
                sp.wait_ge(y_taken, m + 1)
                sp.dma_start(y_v[:, bass.ds(m - TILES, 1), :].rearrange("p o n -> p (o n)"), ys[j % 2])\
                  .then_inc(y_stored[j % 2], 16)
            with sp.Fori(1, TILES // UNROLL) as g:
                for j in range(UNROLL):
                    t = g * UNROLL + j
                    load_block(used + t, xn2_v, t, j)
                    sp.wait_ge(row_added, (t + (1 - UNROLL)) * TOPK)
                    sp.dma_start(out_v[:, t - UNROLL, :], acc[:, t - UNROLL, :]).then_inc(out_stored, 16)
            for t in range(TILES - UNROLL, TILES):
                sp.wait_ge(row_added, (t + 1) * TOPK)
                sp.dma_start(out_v[:, t, :], acc[:, t, :]).then_inc(out_stored, 16)
            sp.wait_ge(out_stored, 16 * TILES)

        @block.tensor
        def _(pe):
            def scores(b):
                pe.wait_ge(q_lo, b + 1)
                pe.wait_ge(ct_split, b * 2 + 2)
                if within(b - 1):
                    pe.wait_ge(sc_taken, b)
                for t in range(TPB):
                    prods = [(q[:, c, t * P:(t + 1) * P], k[:, c, :])
                             for c in range(KC) for q, k in parts3(qt, ct)]
                    for n, (q, k) in enumerate(prods):
                        mm = pe.matmul(ps_sc[:, t, :], q, k, start=n == 0, stop=n == len(prods) - 1)
                mm.then_inc(sc_mm, 1)

            def transpose_x(b):
                pe.wait_ge(xn_ready, b * 2 + 2)
                if within(b - 1):
                    pe.wait_ge(xt_lo, b)
                for t in range(TPB):
                    for c in range(KC):
                        mm = pe.transpose(ps_xt[:, c, t * P:(t + 1) * P], xn[:, t, c * P:(c + 1) * P], ident[:, :])
                mm.then_inc(xt_mm, 1)

            def queries(b):
                if isinstance(b, int) and b == 0:
                    pe.wait_ge(wqo_split, 1)
                pe.wait_ge(xt_lo, b + 1)
                for j in range(KC):
                    prods = [(w[:, c, j * P:(j + 1) * P], a[:, c, :])
                             for c in range(KC) for w, a in parts3(wq, xt)]
                    for n, (w, a) in enumerate(prods):
                        mm = pe.matmul(ps_qo[:, j, :], w, a, start=n == 0, stop=n == len(prods) - 1)
                mm.then_inc(q_mm, 1)

            def transpose_probs(b):
                pe.wait_ge(probs_ready, b * 2 + 2)
                if within(b - 2):
                    pe.wait_ge(rexp_ready, b - 1)
                for t in range(TPB):
                    for c in range(NC):
                        mm = pe.transpose(ps_pt[:, c, t * P:(t + 1) * P], probs[:, t, c * P:(c + 1) * P], ident[:, :])
                mm.then_inc(pt_mm, 1)

            def attend(b):
                pe.wait_ge(pt_lo, b + 1)
                pe.wait_ge(cn_split, b * 2 + 2)
                for j in range(KC):
                    prods = [(v[:, c, j * P:(j + 1) * P], a[:, c, :])
                             for c in range(NC) for v, a in parts3(cn, pt)]
                    for n, (v, a) in enumerate(prods):
                        mm = pe.matmul(ps_qo[:, j, :], v, a, start=n == 0, stop=n == len(prods) - 1)
                mm.then_inc(o_mm, 1)

            def project(b):
                if isinstance(b, int) and b == 0:
                    pe.wait_ge(wqo_split, 2)
                pe.wait_ge(o_lo, b + 1)
                for t in range(TPB):
                    prods = [(o[:, c, t * P:(t + 1) * P], w[:, c, :])
                             for c in range(KC) for o, w in parts3(ot, wo)]
                    for n, (o, w) in enumerate(prods):
                        mm = pe.matmul(ps_y[t], o, w, start=n == 0, stop=n == len(prods) - 1)
                    mm.then_inc(y_mm, 1)

            def transpose_x2(b):
                pe.wait_ge(xn2_ready, b * 2 + 2)
                pe.wait_ge(x1_ready, b * 2 + 2)
                for t in range(TPB):
                    for c in range(KC):
                        mm = pe.transpose(ps_x2[:, c, t * P:(t + 1) * P], xn2[:, t, c * P:(c + 1) * P], ident[:, :])
                mm.then_inc(x2_mm, 1)

            def logits(b):
                pe.wait_ge(x2_taken, b + 1)
                for t in range(TPB):
                    for c in range(KC):
                        mm = pe.matmul(ps_lg[:, t, :], x2[:, c, t * P:(t + 1) * P], raw_gw[:, c, :],
                                       start=c == 0, stop=c == KC - 1)
                mm.then_inc(lg_mm, 1)

            def block_transpose(n, j):
                pe.wait_ge(xb_in[j], ((n - j) // UNROLL + 1) * 16 if isinstance(n, int)
                           else n * (16 // UNROLL) + (16 - j * (16 // UNROLL)))
                if not (isinstance(n, int) and n == 0):
                    pe.wait_ge(bx_lo, n)
                for c in range(KC):
                    mm = pe.transpose(ps_bx[:, c, :], xb[j][:, c * P:(c + 1) * P], ident[:, :])
                mm.then_inc(bx_mm, 1)

            def gate_up(n, j, off):
                pe.wait_ge(bx_lo, n + 1)
                for c in range(KC):
                    for part, (a, weights) in enumerate(((bx[j % 2][0], (0, WSET)), (bx[j % 2][1], (0,)))):
                        for half, bank in ((0, ps_g), (1, ps_u)):
                            for w in weights:
                                at = w + c * 2 * INNER + half * INNER
                                mm = pe.matmul(bank, a[:, c, :], slots[:, bass.ds(off + at, INNER)],
                                               start=c == 0 and part == 0 and w == 0,
                                               stop=c == KC - 1 and part == 1)
                mm.then_inc(gu_mm, 1)

            def hidden_transpose(n):
                pe.wait_ge(hid_ready, n + 1)
                if not (isinstance(n, int) and n == 0):
                    pe.wait_ge(ht_lo, n)
                for c in range(HC):
                    mm = pe.transpose(ps_ht[:, c, :], hid[:, c * P:(c + 1) * P], ident[:, :])
                mm.then_inc(ht_mm, 1)

            def down(n, j, off):
                pe.wait_ge(ht_lo, n + 1)
                if not (isinstance(n, int) and n < 2):
                    pe.wait_ge(y_taken, n - 1)
                for c in range(HC):
                    for part, (a, weights) in enumerate(((hth, (0, WSET)), (htl, (0,)))):
                        for w in weights:
                            at = w + W13 + c * D
                            mm = pe.matmul(ps_y[j % 2], a[:, c, :], slots[:, bass.ds(off + at, D)],
                                           start=c == 0 and part == 0 and w == 0,
                                           stop=c == HC - 1 and part == 1)
                mm.then_inc(down_mm, 1)

            def ranks():
                pe.wait_ge(sel_ready, BATCH)
                flat = sel[:, :, :].rearrange("p t e -> p (t e)")
                flat_rank = ps_rank.rearrange("p t e -> p (t e)")
                pe.matmul(flat_rank, upper[:, :], flat, start=True, stop=False)
                for t in range(TILES - 1):
                    rest = TILES - 1 - t
                    pe.matmul(ps_rank[:, t + 1:TILES, :], ones[:, :], sel[:, t:t + 1, :].broadcast_to([P, rest, EXPERTS]),
                              start=False, stop=False)
                mm = pe.matmul(flat_rank, upper[:, 0:1].broadcast_to([P, P]), flat, start=False, stop=True)
                mm.then_inc(rank_mm, 1)
                for t in range(TILES):
                    mm = pe.matmul(ps_tot, ones[:, :], sel[:, t, :], start=t == 0, stop=t == TILES - 1)
                mm.then_inc(rank_mm, 1)

            def slot_of(n):
                return pe.value_load(slot_tab[0:1, bass.ds(n, 1)], min_val=0, max_val=(SLOTS - 1) * SLOT)

            def sets_of(n):
                return pe.value_load(ready_tab[0:1, bass.ds(n, 1)], min_val=READY, max_val=SETS - 1 + READY)

            def group(g, start=0, static=None):
                before = static if static is not None else slot_of(g * UNROLL - 1)
                for j in range(start, UNROLL):
                    n = g * UNROLL + j
                    here = static
                    if static is None:
                        here = slot_of(n)
                        sets = sets_of(n)
                    block_transpose(n + 1, (j + 1) % UNROLL)
                    hidden_transpose(n - 1)
                    if static is None:
                        pe.wait_ge(w_ready, sets)
                    gate_up(n, j, here)
                    down(n - 1, j - 1, before)
                    before = here

            def iteration(i):
                if within(i - 1):
                    transpose_probs(i - 1)
                if within(i + 2):
                    transpose_x(i + 2)
                if within(i - 2):
                    transpose_x2(i - 2)
                if within(i + 1):
                    scores(i + 1)
                if within(i - 1):
                    attend(i - 1)
                if within(i - 2):
                    logits(i - 2)
                if isinstance(i, int) and i == BATCH:
                    block_transpose(0, 0)
                if within(i - 1):
                    project(i - 1)
                if within(i + 2):
                    queries(i + 2)

            pe.wait_ge(consts_made, 4)
            for i in range(-2, STEADY):
                iteration(i)
            with pe.Fori(STEADY, BATCH - 3) as i:
                iteration(i)
            for i in range(BATCH - 3, BATCH + 1):
                iteration(i)

            pe.wait_ge(first_lo, 2)
            gate_up(0, 0, 0)
            block_transpose(1, 1)
            transpose_x2(BATCH - 1)
            hidden_transpose(0)
            logits(BATCH - 1)
            block_transpose(2, 2)
            ranks()
            gate_up(1, 1, 0)
            down(0, 0, 0)
            group(0, start=2, static=0)
            with pe.Fori(1, TILES // UNROLL) as g:
                group(g, static=0)
            pe.wait_ge(tables_ready, 1)
            with pe.Fori(FIRST_ROUTED, FIRST_SPARE) as g:
                group(g)
            used = load_used(pe)
            with pe.Fori(FIRST_SPARE, END_ROUTED) as g:
                with pe.If(used > g * UNROLL):
                    group(g)
            before = slot_of(used - 1)
            last_slot = (SETS - 1) % SLOTS * SLOT
            pe.wait_ge(w_ready, SETS - 1 + READY)

            def last_blocks(n, j, before, last=False):
                if not last:
                    block_transpose(n + 1, (j + 1) % UNROLL)
                hidden_transpose(n - 1)
                gate_up(n, j, last_slot)
                down(n - 1, j - 1, before)

            for j in range(UNROLL):
                last_blocks(used + j, j, last_slot if j else before)
            with pe.Fori(1, TILES // UNROLL - 1) as g:
                for j in range(UNROLL):
                    last_blocks(used + (g * UNROLL + j), j, last_slot)
            for j in range(UNROLL):
                last_blocks(used + (TILES - UNROLL + j), j, last_slot, last=j == UNROLL - 1)
            hidden_transpose(used + (TILES - 1))
            down(used + (TILES - 1), UNROLL - 1, last_slot)

        @block.scalar
        def _(act):
            step = Steps(act, act_step)

            def hi(dst, src, done):
                act.activation(dst, src, ACT.Copy).then_inc(done, 1)

            def take_scores(b):
                act.wait_ge(sc_mm, b + 1)
                if within(b - 1):
                    act.wait_ge(sc_free, b * 2)
                act.activation(sc, ps_sc, ACT.Copy, scale=coef).then_inc(sc_taken, 1)

            def exponent(b, t):
                act.wait_ge(max_ready, b * 2 + (t + 1))
                if t == 0 and within(b - 1):
                    act.wait_ge(pt_mm, b)
                step.did(act.activation(shifted[:, t, :], sc[:, t, :], ACT.Identity, bias=negmax[:, t:t + 1]))
                step.order()
                act.activation(probs[:, t, :], shifted[:, t, :], ACT.Exp).then_inc(exp_ready, 1)

            def norm_apply(b, dst, rstd, shift, ready, done):
                act.wait_ge(ready, b + 1)
                for t in range(TPB):
                    act.activation(dst[:, t, :], acc[:, b * 2 + t, :], ACT.Identity, scale=rstd[:, t:t + 1],
                                   bias=shift[:, t:t + 1]).then_inc(done, 1)

            def ln1_apply(b):
                if within(b - 1):
                    act.wait_ge(xt_mm, b)
                norm_apply(b, xn, rstd1, shift1, ln1_rstd, xn_ready)

            def ln2_apply(b):
                if within(b - 1):
                    act.wait_ge(x2_mm, b)
                    act.wait_ge(xn2_stored, b * 16)
                norm_apply(b, xn2, rstd2, shift2, ln2_rstd, xn2_ready)

            def take_x2(b):
                act.wait_ge(x2_mm, b + 1)
                if within(b - 1):
                    act.wait_ge(lg_mm, b)
                hi(x2[:, :, :], ps_x2, x2_taken)

            def router_exp(b):
                act.wait_ge(rmax_ready, b + 1)
                for t in range(TPB):
                    last = act.activation(rexp[:, t, :], ps_lg[:, t, :], ACT.Exp, bias=rneg[:, t:t + 1])
                last.then_inc(rexp_ready, 1)

            def tokens_hi(n, j):
                act.wait_ge(bx_mm, n + 1)
                if not (isinstance(n, int) and n < 2):
                    act.wait_ge(gu_mm, n - 1)
                hi(bx[j % 2][0], ps_bx, bx_hi)

            def hidden_hi(n):
                act.wait_ge(ht_mm, n + 1)
                if not (isinstance(n, int) and n == 0):
                    act.wait_ge(down_mm, n)
                hi(hth, ps_ht, ht_hi)

            def gate_silu(n):
                act.wait_ge(gu_mm, n + 1)
                if not (isinstance(n, int) and n == 0):
                    act.wait_ge(hid_ready, n)
                act.activation(silu, ps_g, ACT.Silu).then_inc(silu_ready, 1)

            def next_hi_piece(piece):
                if piece == 0:
                    act.wait_ge(set1_in, 16 + HC * 16)
                src, high, _ = split_piece(1, piece)
                hi(high, src, next_hi)

            def iteration(i):
                if within(i - 1):
                    act.wait_ge(pt_mm, i)
                    if within(i - 2):
                        act.wait_ge(o_mm, i - 1)
                    hi(pt[0], ps_pt, pt_hi)
                if within(i - 2):
                    take_x2(i - 2)
                if within(i + 2):
                    act.wait_ge(xt_mm, i + 3)
                    if within(i + 1):
                        act.wait_ge(q_mm, i + 2)
                    hi(xt[0], ps_xt, xt_hi)
                if isinstance(i, int) and i == -2:
                    hi_of_wo_and_coef()
                if within(i):
                    exponent(i, 0)
                    exponent(i, 1)
                if within(i + 1):
                    take_scores(i + 1)
                if within(i - 1):
                    act.wait_ge(o_mm, i)
                    if within(i - 2):
                        act.wait_ge(y_mm, i * 2 - 2)
                    hi(ot[0], ps_qo, o_hi)
                if isinstance(i, int) and i == BATCH:
                    tokens_hi(0, 0)
                if within(i - 2):
                    router_exp(i - 2)
                if within(i + 3):
                    ln1_apply(i + 3)
                if within(i - 1):
                    ln2_apply(i - 1)
                if within(i + 2):
                    act.wait_ge(q_mm, i + 3)
                    if within(i + 1):
                        act.wait_ge(sc_mm, i + 2)
                    hi(qt[0], ps_qo, q_hi)

            def hi_of_wo_and_coef():
                act.wait_ge(small_in, 16 * 5)
                act.activation(cf[:, 0:1], scal[:, 2:3], ACT.Exp, scale=-1.0)
                act.activation(cf[:, 1:2], scal[:, 3:4], ACT.Exp).then_inc(coef_exp, 1)
                act.wait_ge(wo_in, 16)
                hi(wo[0], raw_o, wqo_hi)
                act.wait_ge(coef_ready, 1)

            act.wait_ge(wq_in, 16)
            hi(wq[0], raw_q, wqo_hi)
            ln1_apply(0)
            for i in range(-2, STEADY):
                iteration(i)
            with act.Fori(STEADY, BATCH - 3) as i:
                step.enter(i, STEADY, TPB)
                iteration(i)
                step.leave(BATCH - 3 - STEADY)
            def first_hi_half(half):
                act.wait_ge(set0_in[half], 16 + half * HC * 16)
                src, high, _ = split_piece(0, half)
                hi(high, src, first_hi)

            first_hi_half(0)
            iteration(BATCH - 3)
            iteration(BATCH - 2)
            iteration(BATCH - 1)
            first_hi_half(1)
            iteration(BATCH)

            def group(g, start=0, last=False, base=0):
                for j in range(start, UNROLL):
                    n = g * UNROLL + j if isinstance(base, int) else base + (g * UNROLL + j)
                    if not (last and j == UNROLL - 1):
                        tokens_hi(n + 1, j + 1)
                    hidden_hi(n - 1)
                    gate_silu(n)
                    if start:
                        next_hi_piece(j)

            gate_silu(0)
            act.wait_ge(y_mm, TILES)
            tokens_hi(1, 1)
            take_x2(BATCH - 1)
            hidden_hi(0)
            router_exp(BATCH - 1)
            tokens_hi(2, 2)
            gate_silu(1)
            next_hi_piece(0)
            next_hi_piece(1)
            group(0, start=2)
            with act.Fori(1, FIRST_SPARE) as g:
                group(g)
            act.wait_ge(tables_ready, 1)
            used = load_used(act)
            with act.Fori(FIRST_SPARE, END_ROUTED) as g:
                with act.If(used > g * UNROLL):
                    group(g)
            with act.Fori(0, TILES // UNROLL - 1) as g:
                group(g, base=used)
            group(TILES // UNROLL - 1, last=True, base=used)
            hidden_hi(used + (TILES - 1))

        @block.vector
        def _(dve):
            step = Steps(dve, dve_step)
            rstep = Steps(dve, router_step)

            def lo(dst, src, high, ready, count, done):
                dve.wait_ge(ready, count)
                dve.tensor_tensor(dst, src, f32(high), ALU.subtract).then_inc(done, 1)

            def norm_stats(b, stats, mv, ve, negm, out_sem):
                step.order()
                step.alone()
                for t in range(TPB):
                    step.did(dve.bn_stats(stats[:, t, :], acc[:, b * 2 + t, :]))
                for t in range(TPB):
                    step.order_before_last()
                    step.alone()
                    step.did(dve.bn_aggr(mv[:, t, :], stats[:, t, :]))
                step.order()
                step.did(dve.tensor_scalar(negm[:, :], mv[:, :, 0], -1.0, None, ALU.mult))
                dve.tensor_scalar(ve[:, :], mv[:, :, 1], EPS, None, ALU.add).then_inc(out_sem, 1)

            def ln1_stats(b):
                if isinstance(b, int) and b <= 3:
                    dve.wait_ge(x_in[b], 16 if b < 3 else 16 * (BATCH - 3))
                if within(b - 1):
                    dve.wait_ge(ln1_rstd, b)
                norm_stats(b, stats1, mv1, ve1, negm1, ln1_var)

            def first_round(b):
                step.order()
                step.alone()
                for t in range(TPB):
                    step.did(dve.max(top8[:, t, :], sc[:, t, :]))
                for t in range(TPB):
                    step.order() if t else step.order_before_last()
                    dve.tensor_scalar(negmax[:, t:t + 1], top8[:, t, 0:1], -1.0, None, ALU.mult)\
                       .then_inc(max_ready, 1)
                step.alone()
                for t in range(TPB):
                    dve.match_replace(left[:, t, :], top8[:, t, :], sc[:, t, :], LOWEST).then_inc(sc_free, 1)

            def top_max(b, r, t):
                if r == 1:
                    dve.wait_ge(sc_free, b * 2 + (t + 1))
                else:
                    step.order_before_last()
                step.alone()
                step.did(dve.max(top8[:, t, :], left[:, t, :]))

            def top_replace(t):
                step.order_before_last()
                step.alone()
                step.did(dve.match_replace(left[:, t, :], top8[:, t, :], left[:, t, :], LOWEST))

            def top_round(b, r):
                for t in range(TPB):
                    top_max(b, r, t)
                for t in range(TPB):
                    top_replace(t)

            def masked_probs(b):
                at = (KEEP - 1) % 8
                dve.wait_ge(max_ready, b * 2 + 2)
                step.order()
                step.did(dve.tensor_tensor(thr[:, :], top8[:, :, at], negmax[:, :], ALU.add))
                step.order()
                for t in range(TPB):
                    dve.wait_ge(exp_ready, b * 2 + (t + 1))
                    dve.scalar_tensor_tensor(out=probs[:, t, :], in0=shifted[:, t, :], scalar=thr[:, t:t + 1],
                                             in1=probs[:, t, :], op0=ALU.is_ge, op1=ALU.mult,
                                             accum_out=psums[:, t:t + 1]).then_inc(probs_ready, 1)

            def sum_inverse(b):
                dve.wait_ge(probs_ready, b * 2 + 2)
                step.did(dve.reciprocal(rinv[:, bass.ds(b * 2, 2)], psums[:, :]))

            def residual(b):
                for t in range(TPB):
                    dve.wait_ge(y_mm, b * 2 + (t + 1))
                    dve.scalar_tensor_tensor(out=acc[:, b * 2 + t, :], in0=ps_y[t], scalar=rinv[:, bass.ds(b * 2 + t, 1)],
                                             in1=acc[:, b * 2 + t, :], op0=ALU.mult, op1=ALU.add)\
                       .then_inc(x1_ready, 1)
                dve.wait_ge(x1_ready, b * 2 + 2)

            def router_max(b):
                dve.wait_ge(lg_mm, b + 1)
                if within(b - 1):
                    dve.wait_ge(sel_ready, b)
                dve.tensor_reduce(rneg[:, :], ps_lg, AX.X, ALU.max, negate=True).then_inc(rmax_ready, 1)

            def router_softmax(b, part):
                if part == 0:
                    dve.wait_ge(rexp_ready, b + 1)
                    rstep.did(dve.tensor_reduce(rsum[:, :], rexp[:, :, :], AX.X, ALU.add))
                elif part == 1:
                    rstep.order()
                    rstep.did(dve.reciprocal(rrec[:, :], rsum[:, :]))
                else:
                    rstep.order()
                    rstep.did(dve.tensor_tensor(rp[:, :, 0:EXPERTS], rexp[:, :, :],
                                                rrec[:, :].unsqueeze(2).broadcast_to([P, TPB, EXPERTS]), ALU.mult))

            def router_top(b, part):
                rstep.order()
                if part == 0:
                    rstep.alone()
                    for t in range(TPB):
                        rstep.did(dve.max(rtop[:, t, :], rp[:, t, 0:EXPERTS]))
                elif part == 1:
                    rstep.did(dve.memset(rtop[:, :, TOPK:8], SENTINEL))
                elif part == 2:
                    rstep.alone()
                    for t in range(TPB):
                        rstep.did(dve.match_replace(rq[:, t, :], rtop[:, t, :], rp[:, t, :], TAKEN))
                    rstep.did(dve.tensor_reduce(rwsum[:, :], rtop[:, :, 0:TOPK], AX.X, ALU.add))

            def router_weights(b, part):
                here = sel[:, bass.ds(b * 2, 2), :]
                rstep.order()
                if part == 0:
                    rstep.did(dve.tensor_scalar(rsum[:, :], rwsum[:, :], 1e-20, None, ALU.add))
                    rstep.did(dve.tensor_scalar(here, rq[:, :, 0:EXPERTS], TAKEN, None, ALU.is_equal))
                elif part == 1:
                    rstep.did(dve.reciprocal(rwrec[:, :], rsum[:, :]))
                    rstep.did(dve.tensor_tensor(rexp[:, :, :], rp[:, :, 0:EXPERTS], here, ALU.mult))
                else:
                    dve.tensor_tensor(comb[:, bass.ds(b * 2, 2), :], rexp[:, :, :],
                                      rwrec[:, :].unsqueeze(2).broadcast_to([P, TPB, EXPERTS]), ALU.mult)\
                       .then_inc(sel_ready, 1)

            def coefficient():
                dve.wait_ge(coef_exp, 1)
                step.did(dve.tensor_scalar(cf[:, 2:3], cf[:, 0:1], 1.0, None, ALU.add))
                step.order()
                step.did(dve.reciprocal(cf[:, 3:4], cf[:, 2:3]))
                step.order()
                step.did(dve.tensor_scalar(cf[:, 4:5], cf[:, 3:4], -1.0, 1.0, ALU.mult, ALU.add))
                step.order()
                step.did(dve.tensor_tensor(cf[:, 5:6], cf[:, 4:5], scal[:, 1:2], ALU.mult))
                step.order()
                step.did(dve.scalar_tensor_tensor(out=cf[:, 6:7], in0=scal[:, 0:1], scalar=cf[:, 3:4], in1=cf[:, 5:6],
                                                  op0=ALU.mult, op1=ALU.add))
                step.order()
                dve.tensor_scalar(coef, cf[:, 6:7], SCALE, cf[:, 1:2], ALU.mult, ALU.mult).then_inc(coef_ready, 1)
            def iteration(i):
                if isinstance(i, int) and i < 0:
                    ln1_stats(i + 3)
                if within(i):
                    dve.wait_ge(sc_taken, i + 1)
                    first_round(i)
                if within(i - 1):
                    lo(pt[1], ps_pt, pt[0], pt_hi, i, pt_lo)
                if isinstance(i, int) and i == BATCH:
                    first_lo_half(1)
                if within(i):
                    top_round(i, 1)
                if within(i + 2):
                    lo(xt[1], ps_xt, xt[0], xt_hi, i + 3, xt_lo)
                if isinstance(i, int) and i == -2:
                    coefficient()
                    lo(wo[1], raw_o, wo[0], wqo_hi, 2, wqo_split)
                if within(i):
                    top_round(i, 2)
                if within(i) and within(i + 2):
                    top_round(i, 3)
                if within(i - 1):
                    lo(ot[1], ps_qo, ot[0], o_hi, i, o_lo)
                if isinstance(i, int) and i == BATCH:
                    tokens_lo(0, 0)
                if within(i) and not within(i + 2):
                    top_round(i, 3)
                if within(i + 3) and not (isinstance(i, int) and i < 0):
                    ln1_stats(i + 3)
                if within(i - 2):
                    router_max(i - 2)
                if within(i):
                    top_round(i, 4)
                if within(i - 1) and not within(i):
                    residual(i - 1)
                    norm_stats(i - 1, stats2, mv2, ve2, negm2, ln2_var)
                if within(i):
                    top_max(i, 5, 0)
                if within(i - 2):
                    router_softmax(i - 2, 0)
                if within(i):
                    top_max(i, 5, 1)
                if within(i - 2):
                    router_softmax(i - 2, 1)
                if within(i):
                    top_replace(0)
                if within(i - 2):
                    router_softmax(i - 2, 2)
                if within(i):
                    top_replace(1)
                if within(i - 2):
                    router_top(i - 2, 0)
                if within(i - 1) and within(i):
                    residual(i - 1)
                    norm_stats(i - 1, stats2, mv2, ve2, negm2, ln2_var)
                if within(i):
                    top_max(i, 6, 0)
                if within(i - 2):
                    router_top(i - 2, 1)
                if within(i):
                    top_max(i, 6, 1)
                if within(i - 2):
                    router_top(i - 2, 2)
                if within(i):
                    masked_probs(i)
                if within(i - 2):
                    router_weights(i - 2, 0)
                if within(i):
                    sum_inverse(i)
                if within(i - 2):
                    router_weights(i - 2, 1)
                if within(i + 2):
                    lo(qt[1], ps_qo, qt[0], q_hi, i + 3, q_lo)
                if within(i - 2):
                    router_weights(i - 2, 2)

            def tokens_lo(n, j):
                lo(bx[j % 2][1], ps_bx, bx[j % 2][0], bx_hi, n + 1, bx_lo)

            def hidden_lo(n):
                lo(htl, ps_ht, hth, ht_hi, n + 1, ht_lo)

            def hidden(n):
                dve.wait_ge(silu_ready, n + 1)
                if not (isinstance(n, int) and n == 0):
                    dve.wait_ge(ht_mm, n)
                dve.tensor_tensor(hid[:, 0:INNER], silu, ps_u, ALU.mult).then_inc(hid_ready, 1)

            def add_tile(n, j, t):
                dve.wait_ge(down_mm, n + 1)
                dve.tensor_tensor(acc[:, t, :], ps_y[j % 2], acc[:, t, :], ALU.add).then_inc(y_taken, 1)

            def take_y(n, j, stores):
                dve.wait_ge(down_mm, n + 1)
                if stores is not None:
                    dve.wait_ge(y_stored[j % 2], stores)
                dve.tensor_copy(ys[j % 2], ps_y[j % 2]).then_inc(y_taken, 1)

            def add_row(n, t, j, k):
                r = (j * TOPK + k) % RING
                uses = UNROLL * TOPK // RING
                nth = (j * TOPK + k) // RING + 1
                dve.wait_ge(gathered[r], (t - j) * (16 * uses // UNROLL) + 16 * nth)
                if k == 0:
                    dve.wait_ge(y_taken, n + 1)
                else:
                    dve.wait_ge(row_added, t * TOPK + k)
                dve.scalar_tensor_tensor(out=acc[:, t, :], in0=ring[r], scalar=wgt[:, t, k:k + 1],
                                         in1=acc[:, t, :], op0=ALU.mult, op1=ALU.add).then_inc(row_added, 1)

            def last_half(n, t, j, rows=True, last=False):
                m = (j - 2) % UNROLL

                def row(k):
                    if rows:
                        add_row(n - 2, t - 2, m, k)

                row(0)
                hidden_lo(n - 1)
                row(1)
                if not last:
                    tokens_lo(n + 1, j + 1)
                row(2)
                hidden(n)
                row(3)
                add_tile(n - 1, (j - 1) % UNROLL, t - 1)
                row(4)
                row(5)

            def front(n, j, last=False):
                if not last:
                    tokens_lo(n + 1, j + 1)
                hidden_lo(n - 1)
                hidden(n)

            def first_lo_half(half):
                dve.wait_ge(first_hi, half + 1)
                src, high, low = split_piece(0, half)
                dve.tensor_tensor(low, src, f32(high), ALU.subtract).then_inc(first_lo, 1)
                if half == 0:
                    dve.wait_ge(first_lo, 1)
                    dve.memset(stage[rest:P, WSET - HALF_A - D:WSET - HALF_A], 0.0).then_inc(pads_zeroed, 1)

            def next_lo_piece(piece):
                dve.wait_ge(next_hi, piece + 1)
                src, high, low = split_piece(1, piece)
                dve.tensor_tensor(low, src, f32(high), ALU.subtract).then_inc(w_ready, 1)

            dve.memset(zeros, 0.0).then_inc(zeros_made, 1)
            step.did(dve.memset(rp[:, :, :], SENTINEL))
            step.did(dve.memset(delta[:, :], float(SLOT)))
            step.order()
            step.did(dve.memset(delta[:, 1:EXPERTS:SLOTS], float(SLOT * (1 - SLOTS))))
            ln1_stats(0)
            lo(wq[1], raw_q, wq[0], wqo_hi, 1, wqo_split)
            for i in range(-2, STEADY):
                iteration(i)
            with dve.Fori(STEADY, BATCH - 3) as i:
                step.enter(i, STEADY, DVE_STEPS)
                rstep.enter(i, STEADY, ROUTER_STEPS)
                iteration(i)
                step.leave(BATCH - 3 - STEADY)
                rstep.leave(BATCH - 3 - STEADY)
            first_lo_half(0)
            iteration(BATCH - 3)
            iteration(BATCH - 2)
            iteration(BATCH - 1)
            iteration(BATCH)
            step.did(dve.memset(hid[:, INNER:HPAD], 0.0))
            step.order()
            hidden(0)
            tokens_lo(1, 1)
            hidden_lo(0)
            iteration(BATCH + 1)
            tokens_lo(2, 2)

            dve.wait_ge(sel_ready, BATCH)
            flat = sel[:, :, :].rearrange("p t e -> p (t e)")
            step.did(dve.tensor_tensor_scan(run[:, :, :].rearrange("p t e -> p (t e)"), flat, flat, 0.0,
                                            ALU.add, ALU.max))
            dve.wait_ge(consts_made, 4)
            dve.wait_ge(rank_mm, 2)
            step.did(dve.tensor_tensor(cmp_e[:, :, :], ps_tot.unsqueeze(2).broadcast_to([P, EXPERTS, EXPERTS]),
                                       blocks_m[:, :].unsqueeze(1).broadcast_to([P, EXPERTS, EXPERTS]), ALU.is_gt))
            step.order()
            step.did(dve.tensor_tensor(pick[:, :, :], run[:, :, :], six_t[:, :, :], ALU.subtract))
            step.did(dve.tensor_reduce(nblk[:, :], cmp_e[:, :, :], AX.X, ALU.add))
            step.order()
            step.did(dve.tensor_tensor(run[:, :, :], pick[:, :, :], sel[:, :, :], ALU.mult))
            step.did(dve.tensor_scalar(nblk1[:, :], nblk[:, :], 1.0, None, ALU.max))
            step.order()
            step.did(dve.tensor_tensor_scan(ends[:, :], nblk1[:, :], nblk1[:, :], 0.0, ALU.add, ALU.max))
            step.order()
            step.did(dve.tensor_tensor(starts[:, :], ends[:, :], nblk1[:, :], ALU.subtract))
            step.order()
            step.did(dve.scalar_tensor_tensor(out=posn[:, :, :], in0=starts[:, :].unsqueeze(1).broadcast_to([P, TILES, EXPERTS]),
                                              scalar=float(P), in1=ps_rank, op0=ALU.mult, op1=ALU.add))
            step.did(dve.tensor_scalar(seq_f[0:1, 0:ROUTED // UNROLL], blk_i[0:1, 0:ROUTED // UNROLL], float(UNROLL),
                                       ends[0:1, EXPERTS - 1:EXPERTS], ALU.mult, ALU.is_lt))
            step.order()
            step.did(dve.memset(ends[:, EXPERTS - 1:EXPERTS], float(ROUTED)))
            for k in range(TOPK + 1):
                if k < TOPK:
                    step.order() if k == 0 else step.order_before_last()
                    step.did(dve.scalar_tensor_tensor(out=picks[k % 3], in0=run[:, :, :], scalar=float(k + 1),
                                                      in1=posn[:, :, :], op0=ALU.is_equal, op1=ALU.mult))
                if k > 0:
                    step.order_before_last() if k < TOPK else step.order()
                    with nc.allow_low_precision(reason="row numbers are exact integers below 2^24"):
                        ins = dve.tensor_reduce(idx[:, :, k - 1], picks[(k - 1) % 3], AX.X, ALU.add)
                    if k == TOPK:
                        ins.then_inc(idx_ready, 1)
                        dve.wait_ge(idx_ready, 1)
                    else:
                        step.did(ins)
            hidden(1)
            add_tile(0, 0, 0)
            front(2, 2)
            next_lo_piece(0)
            next_lo_piece(1)
            add_tile(1, 1, 1)
            next_lo_piece(2)
            step.did(dve.tensor_reduce(slot_f[0:1, 0:1], seq_f[0:1, 0:ROUTED // UNROLL], AX.X, ALU.add))
            step.order()
            step.did(dve.tensor_scalar(used_end[:, :], slot_f[0:1, 0:1], float(UNROLL),
                                       float(EXPERTS - ROUTED), ALU.mult, ALU.add))
            step.order()
            dve.wait_ge(zero_filled, 16 * (ROUTED + EXPERTS) // 8)
            row = cmp_block[0:1, :, :]
            step.did(dve.tensor_tensor(row, ends[0:1, :].unsqueeze(1).broadcast_to([1, ROUTED, EXPERTS]),
                                       blk_i[0:1, :].unsqueeze(2).broadcast_to([1, ROUTED, EXPERTS]), ALU.is_le))
            step.order()
            step.did(dve.tensor_reduce(seq_f[0:1, :], row, AX.X, ALU.add))
            step.order()
            step.did(dve.tensor_tensor(row, row, delta[0:1, :].unsqueeze(1).broadcast_to([1, ROUTED, EXPERTS]), ALU.mult))
            step.order()
            step.did(dve.tensor_reduce(slot_f[0:1, :], row, AX.X, ALU.add))
            step.did(dve.memset(slot_tab[:, 0:TILES], 0))
            step.did(dve.memset(ready_tab[:, 0:TILES], READY))
            step.did(dve.memset(slot_tab[:, TILES + ROUTED:BLOCKS], (SETS - 1) % SLOTS * SLOT))
            step.did(dve.memset(ready_tab[:, TILES + ROUTED:BLOCKS], SETS - 1 + READY))
            step.order()
            step.did(dve.tensor_scalar(slot_tab[:, TILES:TILES + ROUTED], slot_f[0:1, :], float(SLOT), None, ALU.add))
            step.did(dve.tensor_scalar(ready_tab[:, TILES:TILES + ROUTED], seq_f[0:1, :], float(READY + 1), None, ALU.add))
            step.order()
            ins = dve.tensor_scalar(end_tab[:, :], ends[0:1, :], float(TILES), None, ALU.add)
            ins.then_inc(tables_ready, 1)
            front(3, 3)
            add_tile(2, 2, 2)
            next_lo_piece(3)
            for k in range(TOPK):
                step.did(dve.scalar_tensor_tensor(out=pick[:, :, :], in0=run[:, :, :], scalar=float(k + 1), in1=comb[:, :, :],
                                                  op0=ALU.is_equal, op1=ALU.mult))
                step.order()
                step.did(dve.tensor_reduce(wgt[:, :, k], pick[:, :, :], AX.X, ALU.add))
                step.order()
            with dve.Fori(1, TILES // UNROLL) as g:
                for j in range(UNROLL):
                    n = g * UNROLL + j
                    front(n, j)
                    add_tile(n - 1, j + UNROLL - 1, n - 1)
            first = FIRST_ROUTED
            for j in range(UNROLL):
                n = first * UNROLL + j
                front(n, j)
                if j == 0:
                    add_tile(n - 1, UNROLL - 1, n - 1)
                else:
                    take_y(n - 1, j - 1, None if j < 3 else 16)

            def routed_group(g):
                for j in range(UNROLL):
                    n = g * UNROLL + j
                    front(n, j)
                    m = (j - 1) % UNROLL
                    done = (g - first) * 2 + (m // 2 if j else m // 2 - 2)
                    take_y(n - 1, m, done * 16)

            with dve.Fori(first + 1, FIRST_SPARE) as g:
                routed_group(g)
            used = load_used(dve)
            with dve.Fori(FIRST_SPARE, END_ROUTED) as g:
                with dve.If(used > g * UNROLL):
                    routed_group(g)
            front(used, 0)
            take_y(used - 1, UNROLL - 1, used * (16 // 2) - (TILES // 2 + 1) * 16)
            for j in range(1, UNROLL):
                last_half(used + j, j, j, rows=j >= 2)
            with dve.Fori(1, TILES // UNROLL - 1) as g:
                for j in range(UNROLL):
                    last_half(used + (g * UNROLL + j), g * UNROLL + j, j)
            for j in range(UNROLL):
                t = TILES - UNROLL + j
                last_half(used + t, t, j, last=j == UNROLL - 1)
            hidden_lo(used + (TILES - 1))
            for k in range(TOPK):
                add_row(used + (TILES - 2), TILES - 2, UNROLL - 2, k)
            add_tile(used + (TILES - 1), UNROLL - 1, TILES - 1)
            for k in range(TOPK):
                add_row(used + (TILES - 1), TILES - 1, UNROLL - 1, k)

        @block.gpsimd
        def _(pool):
            step = Steps(pool, pool_step)

            def split_ctx_t(b):
                pool.wait_ge(ctx_t_in, b * 16 + 16)
                if not (isinstance(b, int) and b == 0):
                    pool.wait_ge(sc_mm, b)
                step.alone()
                pool.tensor_copy(ct[0], raw_ct).then_inc(ct_split, 1)
                pool.wait_ge(ct_split, b * 2 + 1)
                pool.tensor_tensor(ct[1], raw_ct, f32(ct[0]), ALU.subtract).then_inc(ct_split, 1)

            def split_ctx_n(b):
                pool.wait_ge(ctx_n_in, b * 16 + 16)
                if not (isinstance(b, int) and b == 0):
                    pool.wait_ge(o_mm, b)
                step.alone()
                pool.tensor_copy(cn[0], raw_cn).then_inc(cn_split, 1)
                pool.wait_ge(cn_split, b * 2 + 1)
                pool.tensor_tensor(cn[1], raw_cn, f32(cn[0]), ALU.subtract).then_inc(cn_split, 1)

            def root(b, var, ve, negm, rstd, shift, done):
                pool.wait_ge(var, b + 1)
                step.did(pool.tensor_tensor(rstd[:, :], ve[:, :], neghalf[:, :], ALU.pow))
                step.order()
                pool.tensor_tensor(shift[:, :], negm[:, :], rstd[:, :], ALU.mult).then_inc(done, 1)

            def root1(b):
                if within(b - 1):
                    pool.wait_ge(xn_ready, b * 2)
                root(b, ln1_var, ve1, negm1, rstd1, shift1, ln1_rstd)

            def root2(b):
                root(b, ln2_var, ve2, negm2, rstd2, shift2, ln2_rstd)

            def iteration(i):
                if isinstance(i, int) and i < 0:
                    root1(i + 3)
                if within(i + 2):
                    split_ctx_t(i + 2)
                if within(i + 3) and not (isinstance(i, int) and i < 0):
                    root1(i + 3)
                if within(i):
                    split_ctx_n(i)
                if within(i - 1):
                    root2(i - 1)

            step.did(pool.memset(ident[:, :], 0.0))
            step.did(pool.memset(upper[:, :], 1.0))
            step.did(pool.memset(neghalf[:, :], -0.5))
            step.order()
            pool.affine_select(out=ident[:, :], in_=ident[:, :], compare_op=ALU.not_equal, fill=1.0,
                               base=0, pattern=[[-1, P]], channel_multiplier=1).then_inc(consts_made, 1)
            pool.affine_select(out=upper[:, :], in_=upper[:, :], compare_op=ALU.is_gt, fill=0.0,
                               base=0, pattern=[[1, P]], channel_multiplier=-1).then_inc(consts_made, 1)
            root1(0)
            pool.memset(ones[:, :], 1.0)
            pool.iota(blk_i[:, :], [[1, ROUTED]], base=0, channel_multiplier=0, allow_small_or_imprecise_dtypes=True)
            pool.iota(blocks_m[:, :], [[P, EXPERTS]], base=0, channel_multiplier=0, allow_small_or_imprecise_dtypes=True)\
                .then_inc(consts_made, 1)
            pool.iota(six_t[:, :, :], [[TOPK, TILES], [0, EXPERTS]], base=0, channel_multiplier=0,
                      allow_small_or_imprecise_dtypes=True).then_inc(consts_made, 1)
            for i in range(-2, STEADY):
                iteration(i)
            with pool.Fori(STEADY, BATCH - 3) as i:
                step.enter(i, STEADY, TPB)
                iteration(i)
                step.leave(BATCH - 3 - STEADY)
            for i in range(BATCH - 3, BATCH):
                iteration(i)

            def load_weights(up, dn, e):
                pool.dma_start(raw[:, 0:W13], up[:, e, :]).then_inc(w_in, 16)
                for c in range(HC):
                    rows = P if c < HC - 1 else rest
                    pool.dma_start(raw[0:rows, W13 + c * D:W13 + (c + 1) * D],
                                   dn[c * P:c * P + rows, e, :]).then_inc(w_in, 16)

            def split_weights(n):
                at = (n % SLOTS if isinstance(n, int) else 0) * SLOT
                split_into(n, at)

            def split_into(n, at):
                if isinstance(n, int) and n == 2:
                    pool.wait_ge(set2_in, 64)
                else:
                    pool.wait_ge(w_in, n * 64 - 128)
                step.alone()
                step.did(pool.tensor_copy(slots[:, at:at + WSET], raw[:, :]))
                step.order()
                pool.tensor_tensor(slots[:, at + WSET:at + SLOT], raw[:, :], f32(slots[:, at:at + WSET]), ALU.subtract)\
                    .then_inc(w_ready, 1)
                pool.wait_ge(w_ready, n + READY)

            pool.wait_ge(ln2_rstd, BATCH - 1)
            pool.wait_ge(cn_split, 2 * BATCH)
            pool.wait_ge(first_lo, 2)
            pool.memset(raw[rest:P, W13 + (HC - 1) * D:WSET], 0.0).then_inc(pads_zeroed, 1)
            pool.wait_ge(pads_zeroed, 2)
            root2(BATCH - 1)

            pool.wait_ge(idx_ready, 1)
            pool.wait_ge(zero_filled, 16 * (ROUTED + EXPERTS) // 8)

            def rows_of_two(g, j):
                step.alone()
                step.did(pool.tensor_copy(idx_now[j // 2][:, :, :], idx[:, bass.ds(g * UNROLL + j, 2), :]))

            def scatter(g, first=False):
                for j in range(UNROLL):
                    if j % 2 == 0:
                        if not first:
                            for last in (j, j + 1):
                                pool.wait_ge(scattered[last], g * (16 * TOPK))
                        rows_of_two(g, j)
                    pool.wait_ge(xb_in[j], g * 16 + 16)
                    step.order()
                    step.alone()
                    for k in range(TOPK):
                        pool.indirect_dma_start(sorted_dram[:, :], bass.IndirectOffsetOnAxis(idx_now[j // 2][:, j % 2, k:k + 1], 0),
                                                xb[j], None).then_inc(scattered[j], 16)
            scatter(0, first=True)
            with pool.Fori(1, TILES // UNROLL) as g:
                step.enter(g, 1, UNROLL // 2)
                scatter(g)
                step.leave(TILES // UNROLL - 1)
            split_into(2, 2 * SLOT)
            load_weights(w13_v, w2_v, 2)
            pool.wait_ge(down_mm, TILES)
            split_into(3, 0)
            load_weights(w13_v, w2_v, 3)
            pool.wait_ge(tables_ready, 1)
            with pool.Fori(0, 4) as m:
                step.enter(m, 0, SLOTS)
                for s in range(SLOTS):
                    n = m * SLOTS + (4 + s)
                    done = pool.value_load(end_tab[0:1, bass.ds(m * SLOTS + s, 1)], min_val=TILES + 1, max_val=TILES + ROUTED)
                    pool.wait_ge(down_mm, done)
                    split_into(n, (4 + s) % SLOTS * SLOT)
                    load_weights(w13_v, w2_v, n)
                step.leave(4)
            for n in (16, 17):
                done = pool.value_load(end_tab[0:1, n - 4:n - 3], min_val=TILES + 1, max_val=TILES + ROUTED)
                pool.wait_ge(down_mm, done)
                split_into(n, n % SLOTS * SLOT)
                if n == 16:
                    load_weights(sw13_v, sw2_v, 1)

            used = load_used(pool)
            for j in range(2):
                pool.wait_ge(y_stored[j], used * (16 // 2) - TILES * (16 // 2))
            def gather(g, first=False):
                for j in range(UNROLL):
                    if j % 2 == 0:
                        rows_of_two(g, j)
                    step.order()
                    for k in range(TOPK):
                        i = j * TOPK + k
                        if not (first and i < RING):
                            pool.wait_ge(row_added, g * (UNROLL * TOPK) + (i - RING + 1))
                        step.alone()
                        pool.indirect_dma_start(ring[i % RING], None, y_dram[:, :],
                                                bass.IndirectOffsetOnAxis(idx_now[j // 2][:, j % 2, k:k + 1], 0))\
                            .then_inc(gathered[i % RING], 16)
            gather(0, first=True)
            with pool.Fori(1, TILES // UNROLL) as g:
                step.enter(g, 1, UNROLL // 2)
                gather(g)
                step.leave(TILES // UNROLL - 1)


def kernel(**inputs):
    import numpy as _np
    import concourse.bacc as _bacc
    from concourse import mybir as _mybir
    from concourse.bass_utils import run_bass_kernel_spmd as _run

    def chunks(a, last):
        lead = a.shape[:-2]
        a = a.reshape(-1, KC, P, last).transpose(0, 2, 1, 3)
        return _np.ascontiguousarray(a).reshape(-1, KC * last)

    g = {k: _np.asarray(v) for k, v in inputs.items()}
    ctx = g["ctx_2048"]
    sw13 = g["L0_ffn_sw13"].reshape(2, 2, INNER, D).transpose(1, 3, 0, 2)
    arrays = {
        "x": g["x"].reshape(TOKENS, D),
        "ctx_n": ctx.reshape(TOKENS, D),
        "ctx_t": chunks(ctx.transpose(0, 2, 1), SEQ),
        "wq_t": chunks(g["L0_xattn_W_qkv"][:D].T[None], D),
        "wo_t": chunks(g["L0_xattn_W_o"].T[None], D),
        "beta_q": g["L0_xattn_beta_q"].reshape(1, 1),
        "beta_k": g["L0_xattn_beta_k"].reshape(1, 1),
        "gate": g["L0_xattn_gate"].reshape(1, 1),
        "log_tau": g["L0_xattn_log_tau"].reshape(1, 1),
        "gate_w_t": g["L0_ffn_gate_w"].T,
        "w13": chunks(g["L0_ffn_w13"].transpose(0, 2, 1), 2 * INNER),
        "w2": g["L0_ffn_w2"].transpose(0, 2, 1).reshape(EXPERTS * INNER, D),
        "sw13": chunks(sw13.reshape(2, D, 2 * INNER), 2 * INNER),
        "sw2": g["L0_ffn_sw2"].T,
    }
    arrays = {k: _np.ascontiguousarray(v) for k, v in arrays.items()}
    nc = _bacc.Bacc("TRN2", target_bir_lowering=False, num_devices=1)
    args = [nc.dram_tensor(k, v.shape, _mybir.dt.from_np(v.dtype), kind="ExternalInput").ap()
            for k, v in arrays.items()]
    args.append(nc.dram_tensor("out", (TOKENS, D), _mybir.dt.float32, kind="ExternalOutput").ap())
    xattn_moe(nc, *args)
    r = _run(nc, [arrays], core_ids=[0])
    return r.results[0]["out"].reshape(BATCH, SEQ, D)
```
